# Optimizing a Trainium2 kernel written in Bass

```python
import numpy as np
import jax
import jax.numpy as jnp

def _softmax(x, axis=-1):
    return jax.nn.softmax(x, axis=axis)

def _gelu(x):
    return jax.nn.gelu(x, approximate=True)

def _silu(x):
    return jax.nn.silu(x)

def _sigmoid(x):
    return jax.nn.sigmoid(x)

def _layernorm(x, axis=-1, eps=1e-05):
    m = jnp.mean(x, axis=axis, keepdims=True)
    v = jnp.var(x, axis=axis, keepdims=True)
    return (x - m) / jnp.sqrt(v + eps)

def _scatter_add(tgt, idx, src, axis=0):
    return tgt.at[idx].add(src)

def _segment_sum(src, seg, n):
    return jax.ops.segment_sum(src, seg, n)
kernel_name = 'mk_hybrid_d1_jaxref_r4_43a904'

def setup_inputs(seed: int=0):
    np.random.seed(seed)
    _w = jnp.asarray

    def _L0_attn_a_setup():
        import jax, jax.numpy as jnp
        import numpy as np
        HIDDEN = 512
        NUM_HEADS = 16
        HEAD_DIM = HIDDEN // NUM_HEADS
        key = jax.random.key(seed)
        ks = jax.random.split(key, 5)
        B, S, H = (2, 512, HIDDEN)
        qkv_bound = float(np.sqrt(6.0 / (H + 3 * H)))
        out_bound = float(np.sqrt(6.0 / (H + H)))
        return {'x': jax.random.normal(ks[0], (B, S, H), dtype=jnp.float32), 'W_qkv': jax.random.uniform(ks[1], (3 * H, H), minval=-qkv_bound, maxval=qkv_bound, dtype=jnp.float32), 'b_qkv': jnp.zeros((3 * H,), dtype=jnp.float32), 'W_out': jax.random.uniform(ks[2], (H, H), minval=-out_bound, maxval=out_bound, dtype=jnp.float32), 'b_out': jnp.zeros((H,), dtype=jnp.float32)}
    _L0_attn_a_in = _L0_attn_a_setup()

    def _L0_attn_b_setup():
        import jax, jax.numpy as jnp
        import numpy as np
        B, T, C = (4, 512, 512)
        NUM_HEADS = 16
        HEAD_SIZE = C // NUM_HEADS
        key = jax.random.key(seed)
        ks = jax.random.split(key, 5)
        scale = 0.02
        return {'x': jax.random.normal(ks[0], (B, T, C), dtype=jnp.float32), 'w_qkv': jax.random.normal(ks[1], (C, 3 * NUM_HEADS * HEAD_SIZE), dtype=jnp.float32) * scale, 'b_qkv': jax.random.normal(ks[2], (3 * NUM_HEADS * HEAD_SIZE,), dtype=jnp.float32) * scale, 'w_proj': jax.random.normal(ks[3], (NUM_HEADS * HEAD_SIZE, C), dtype=jnp.float32) * scale, 'b_proj': jax.random.normal(ks[4], (C,), dtype=jnp.float32) * scale}
    _L0_attn_b_in = _L0_attn_b_setup()

    def _L0_ffn_setup():
        import jax, jax.numpy as jnp
        import numpy as np
        DIM_IN = 512
        DIM_HIDDEN = 2048
        key = jax.random.key(seed)
        k_x, k_g, k_u, k_d = jax.random.split(key, 4)
        s_in = 1.0 / np.sqrt(DIM_IN)
        s_hid = 1.0 / np.sqrt(DIM_HIDDEN)
        x = jax.random.normal(k_x, (4, 512, DIM_IN), dtype=jnp.float32)
        w_gate = jax.random.uniform(k_g, (DIM_HIDDEN, DIM_IN), jnp.float32, -s_in, s_in)
        w_up = jax.random.uniform(k_u, (DIM_HIDDEN, DIM_IN), jnp.float32, -s_in, s_in)
        w_down = jax.random.uniform(k_d, (DIM_IN, DIM_HIDDEN), jnp.float32, -s_hid, s_hid)
        return {'x': x, 'w_gate': w_gate, 'w_up': w_up, 'w_down': w_down}
    _L0_ffn_in = _L0_ffn_setup()
    _d = {'L0_attn_a_x': _L0_attn_a_in['x'], 'L0_attn_a_W_qkv': _L0_attn_a_in['W_qkv'], 'L0_attn_a_b_qkv': _L0_attn_a_in['b_qkv'], 'L0_attn_a_W_out': _L0_attn_a_in['W_out'], 'L0_attn_a_b_out': _L0_attn_a_in['b_out'], 'L0_attn_b_w_qkv': _L0_attn_b_in['w_qkv'], 'L0_attn_b_b_qkv': _L0_attn_b_in['b_qkv'], 'L0_attn_b_w_proj': _L0_attn_b_in['w_proj'], 'L0_attn_b_b_proj': _L0_attn_b_in['b_proj'], 'L0_ffn_w_gate': _L0_ffn_in['w_gate'], 'L0_ffn_w_up': _L0_ffn_in['w_up'], 'L0_ffn_w_down': _L0_ffn_in['w_down']}
    _x0 = _d['L0_attn_a_x']
    _d['L0_attn_a_x'] = jax.random.normal(jax.random.fold_in(jax.random.key(seed), 1), (2, 1024, 512), dtype=_x0.dtype)
    del _x0
    return _d

def reference(L0_attn_a_x, L0_attn_a_W_qkv, L0_attn_a_b_qkv, L0_attn_a_W_out, L0_attn_a_b_out, L0_attn_b_w_qkv, L0_attn_b_b_qkv, L0_attn_b_w_proj, L0_attn_b_b_proj, L0_ffn_w_gate, L0_ffn_w_up, L0_ffn_w_down):

    def _L0_attn_a_ref(x, W_qkv, b_qkv, W_out, b_out):
        import jax, jax.numpy as jnp
        import numpy as np
        HIDDEN = 512
        NUM_HEADS = 16
        HEAD_DIM = HIDDEN // NUM_HEADS
        B, S, H = x.shape
        qkv = x @ W_qkv.T + b_qkv
        q, k, v = jnp.split(qkv, 3, axis=-1)

        def to_heads(t):
            return t.reshape(B, S, NUM_HEADS, HEAD_DIM).transpose(0, 2, 1, 3)
        q, k, v = (to_heads(q), to_heads(k), to_heads(v))
        scale = HEAD_DIM ** (-0.5)
        scores = jnp.einsum('bnqd,bnkd->bnqk', q, k) * scale
        causal = jnp.triu(jnp.ones((S, S), dtype=bool), k=1)
        scores = jnp.where(causal, -jnp.inf, scores)
        attn = jax.nn.softmax(scores, axis=-1)
        out = jnp.einsum('bnqk,bnkd->bnqd', attn, v)
        out = out.transpose(0, 2, 1, 3).reshape(B, S, H)
        return out @ W_out.T + b_out

    def _L0_attn_b_ref(x, w_qkv, b_qkv, w_proj, b_proj):
        import jax, jax.numpy as jnp
        import numpy as np
        B, T, C = (4, 512, 512)
        NUM_HEADS = 16
        HEAD_SIZE = C // NUM_HEADS
        b, t, c = x.shape
        h, d = (NUM_HEADS, HEAD_SIZE)
        qkv = x @ w_qkv + b_qkv
        q, k, v = jnp.split(qkv, 3, axis=-1)
        q = q.reshape(b, t, h, d).transpose(0, 2, 1, 3)
        k = k.reshape(b, t, h, d).transpose(0, 2, 1, 3)
        v = v.reshape(b, t, h, d).transpose(0, 2, 1, 3)
        scores = jnp.einsum('bhqd,bhkd->bhqk', q, k) * d ** (-0.5)
        causal = jnp.tril(jnp.ones((t, t), dtype=bool))
        scores = jnp.where(causal, scores, jnp.float32(-jnp.inf))
        attn = jax.nn.softmax(scores, axis=-1)
        out = jnp.einsum('bhqk,bhkd->bhqd', attn, v)
        out = out.transpose(0, 2, 1, 3).reshape(b, t, h * d)
        return out @ w_proj + b_proj

    def _L0_ffn_ref(x, w_gate, w_up, w_down):
        import jax, jax.numpy as jnp
        import numpy as np
        DIM_IN = 512
        DIM_HIDDEN = 2048
        gate = jnp.einsum('bsd,hd->bsh', x, w_gate)
        up = jnp.einsum('bsd,hd->bsh', x, w_up)
        gated = jax.nn.silu(gate) * up
        return jnp.einsum('bsh,dh->bsd', gated, w_down)
    x = L0_attn_a_x
    x = x + _L0_attn_a_ref(_layernorm(x, axis=-1), L0_attn_a_W_qkv, L0_attn_a_b_qkv, L0_attn_a_W_out, L0_attn_a_b_out)
    x = x + _L0_ffn_ref(_layernorm(x, axis=-1), L0_ffn_w_gate, L0_ffn_w_up, L0_ffn_w_down)
    x = x + _L0_attn_b_ref(_layernorm(x, axis=-1), L0_attn_b_w_qkv, L0_attn_b_b_qkv, L0_attn_b_w_proj, L0_attn_b_b_proj)
    x = x + _L0_ffn_ref(_layernorm(x, axis=-1), L0_ffn_w_gate, L0_ffn_w_up, L0_ffn_w_down)
    return x

_drawn_inputs = setup_inputs


def setup_inputs(seed=0):
    import zlib

    import numpy as np

    out = dict(_drawn_inputs(seed))
    spreads = {'L0_attn_a_b_qkv': (0.0, 0.1), 'L0_attn_a_b_out': (0.0, 0.1)}
    factors = {'L0_attn_b_b_qkv': 6.516, 'L0_attn_b_b_proj': 2.991}
    for name, (base, spread) in spreads.items():
        noise = np.random.default_rng([zlib.crc32(name.encode()), seed]).standard_normal(out[name].shape)
        drawn = base * np.exp(spread * noise) if base else spread * noise
        out[name] = jnp.asarray(drawn.astype(out[name].dtype))
    for name, factor in factors.items():
        out[name] = (out[name] * factor).astype(out[name].dtype)
    return out
```

```python
from contextlib import ExitStack

import concourse.bass as bass
from concourse import mybir

F32 = mybir.dt.float32
F32R = mybir.dt.float32r
BF16 = mybir.dt.bfloat16
ALU = mybir.AluOpType
ACT = mybir.ActivationFunctionType

P = 128
BATCH, TOKENS, DIM, HIDDEN, HEADS = 2, 1024, 512, 2048, 16
LAYERS = 2
HEAD = DIM // HEADS
SCALE = float(HEAD) ** -0.5
EPS = 1e-5
KT = DIM // P
TT = TOKENS // P
CHUNK = 512
CT = CHUNK // P
CHUNKS = TOKENS // CHUNK
GH = P // HEAD
GROUPS = HEADS // GH
UNITS = GROUPS * CHUNKS
BLOCK = 256
BT = BLOCK // P
BLOCKS = HIDDEN // BLOCK
STEPS = BLOCKS * CHUNKS

SLOT = 1024
V_SLOTS, QK_SLOT0, WO_SLOT0, FFN_SLOT0 = (0, 1), 2, 2 + GROUPS, 4 + GROUPS
SLOTS = FFN_SLOT0 + 3 * BLOCKS
RING_SLOTS = 5
SHIFT_AT, SHIFT = WO_SLOT0, (-SLOTS) % RING_SLOTS


def place(i):
    return (i + (SHIFT if i >= SHIFT_AT else 0)) % RING_SLOTS


def slot_before(i):
    return max((j for j in range(i) if place(j) == place(i)), default=None)


def unit(u):
    return u // CHUNKS, u % CHUNKS


def key_tiles(u):
    return CT * (unit(u)[1] + 1)


def downs_after(s):
    return {0: (), STEPS - 2: (s - 1, s), STEPS - 1: (s,)}.get(s, (s - 1,))


def ring_order():
    yield from (("ln1", 0), ("ln1", 1), ("v", 0), ("v", 1), ("proj", 0))
    yield from (("ln1", 2), ("ln1", 3), ("v", 2), ("v", 3))
    for u in range(UNITS):
        if u:
            yield ("proj", u)
        yield from (("s1", u, s) for s in range(GH * CT))
        yield ("mt", u)
    yield from (("ln2", 0), ("ln2", 1))
    for x in range(STEPS):
        yield from (("gu", x, t) for t in range(BT))
        if x == 0:
            yield from (("ln2", 2), ("ln2", 3))


RING = {name: n for n, name in enumerate(ring_order())}
RING_USES = len(RING)
assert RING_USES % 2 == 0 and SLOTS % 2 == 0
J_BASE = [sum(key_tiles(v) for v in range(u)) for u in range(UNITS)]
KEY_STEPS = sum(key_tiles(u) for u in range(UNITS))
S2_STEPS = GH * KEY_STEPS
ROWS = TT + STEPS * CT
HID_TILES = STEPS * BT
STACKED = ((0, 2), (0, 3), (1, 2))


def block_kernel(nc, x_in, attn_w, ffn_w, qk_bias, row_bias, out):
    with ExitStack() as ctx:
        def sb(name, shape, dt=F32):
            return ctx.enter_context(nc.sbuf_tensor(name, shape, dt))

        def sem(name):
            return ctx.enter_context(nc.semaphore(name))

        x = sb("x", [P, TT, DIM])
        xt_hi = sb("xt_hi", [P, KT, TOKENS], F32R)
        xt_lo = sb("xt_lo", [P, KT, TOKENS], F32R)
        v = sb("v", [P, TT, DIM])
        attn = sb("attn", [P, GROUPS, TOKENS])
        kq_stack = sb("kq_stack", [P, 5, GH, CHUNK], F32R)
        k_stack = kq_stack[:, 0:3, :, :]
        q_stack = kq_stack[:, 3:5, :, :]
        h_parts = q_stack.rearrange("p b (s t) n -> p b s t n", s=2)
        prob = sb("prob", [P, 2, GH, CHUNK])
        silu = prob[:, 0, 0:2, :]
        hidden = prob[:, 1, 0:2, :]
        kq_parts = sb("kq_parts", [P, 4, CHUNK], F32R)
        mask_row = sb("mask_row", [P, TOKENS], BF16)
        xn = sb("xn", [P, 2, DIM])
        sum_out = xn[:, :, :].bitcast(BF16)
        w_hi = sb("w_hi", [P, RING_SLOTS, SLOT], F32R)
        w_lo = sb("w_lo", [P, RING_SLOTS, SLOT], F32R)
        w_stage = sb("w_stage", [P, 2, SLOT])
        recip = sb("recip", [P, CHUNK])
        bias_rows = sb("bias_rows", [P, 2, DIM])
        bias_qk = sb("bias_qk", [P, 2, GROUPS])
        ident = sb("ident", [P, P])
        ones = sb("ones", [P, HEAD])
        row_max = sb("row_max", [P, 2, GH * CT])
        nm_hi = sb("nm_hi", [GH * CT, P], F32R)
        nm_lo = sb("nm_lo", [GH * CT, P], F32R)
        stats = sb("stats", [P, TT, 6])
        mean_var = sb("mean_var", [P, TT, 2])
        var_eps = sb("var_eps", [P, TT])
        rstd = sb("rstd", [P, TT])
        minus_half = sb("minus_half", [P, CT])

        ring = [ctx.enter_context(nc.psum_tensor(f"ring{i}", [P, 2, CHUNK], F32)) for i in range(2)]
        bank = [ctx.enter_context(nc.psum_tensor(f"bank{i}", [P, CHUNK], F32)) for i in range(4)]
        out_bank, den_bank = bank[2], bank[3]

        x_loaded, x_stored = ([sem(f"x_{what}{c}") for c in range(CHUNKS)] for what in ("loaded", "stored"))
        bias_loaded = sem("bias_loaded")
        w_loaded = [sem("w_loaded0"), sem("w_loaded1")]
        kq_stacked = [[sem(f"kq_stacked{n}_{h}") for h in range(GH)] for n in range(2)]
        max_stacked = [sem("max_stacked0"), sem("max_stacked1")]
        const_ready, w_split, w_hi_done = sem("const_ready"), sem("w_split"), sem("w_hi_done")
        rstd_ready, out_bias_added, mask_done = sem("rstd_ready"), sem("out_bias_added"), sem("mask_done")
        ring_full, s2_full, pv_done, rows_full = sem("ring_full"), sem("s2_full"), sem("pv_done"), sem("rows_full")
        xt_hi_ready, qk_hi_ready, prob_ready, silu_ready = (
            sem("xt_hi_ready"), sem("qk_hi_ready"), sem("prob_ready"), sem("silu_ready"))
        ring_drained, stats_done, var_ready, xn_ready = (
            sem("ring_drained"), sem("stats_done"), sem("var_ready"), sem("xn_ready"))
        max_ready, nm_hi_done, max_split, recip_done = (
            sem("max_ready"), sem("nm_hi_done"), sem("max_split"), sem("recip_done"))
        attn_ready, attn_hi_done, attn_split = sem("attn_ready"), sem("attn_hi_done"), sem("attn_split")
        h_hi_done, h_ready, rows_drained = sem("h_hi_done"), sem("h_ready"), sem("rows_drained")

        RING_CREDIT = 2

        def buffer_of(name):
            return ring[RING[name] % 2]

        def full(it, name):
            return it * RING_USES + RING[name] + 1

        def drained(it, name):
            return it * RING_USES + RING[name] + 1 + RING_CREDIT

        def buffer_free(it, name):
            return it * RING_USES + RING[name] - 1 + RING_CREDIT

        def stacked(it, u, each):
            return 16 * each * (it * (UNITS // 2) + u // 2 + 1)

        CONSTS = 5

        def wait_alone(eng, semaphore, value):
            if not isinstance(value, int):
                value = eng.snap(eng.to_reg(value))
            eng.wait_ge(const_ready, CONSTS)
            eng.wait_ge(semaphore, value)

        block = ctx.enter_context(nc.Block())

        @block.sync
        def _(sp):
            def load_weights(i, it, attn_src):
                if i >= 2 or it is not None:
                    wait_alone(sp, w_split, (0 if it is None else it * SLOTS) + i - 1)
                j = i % SLOTS
                src = attn_src[j] if j < FFN_SLOT0 else ffn_w[j - FFN_SLOT0]
                sp.dma_start(w_stage[:, j % 2, :], src).then_inc(w_loaded[j % 2], 16)

            def load_biases(layer):
                sp.dma_start(bias_qk[:, :, :], qk_bias[layer]).then_inc(bias_loaded, 16)
                for r in range(2):
                    sp.dma_start(bias_rows[:, r, :], row_bias[layer, r:r + 1, :].to_broadcast([P, DIM])
                                 ).then_inc(bias_loaded, 16)

            def stack_qk(it, u):
                wait_alone(sp, ring_drained, drained(it, ("proj", u)))
                kb, qb = u % 3, 3 + u % 2
                for h in range(GH):
                    rows = slice(h * HEAD, (h + 1) * HEAD)
                    for n, (k, q) in enumerate(STACKED):
                        src = kq_parts[rows, k:q + 1:q - k, :].bitcast(F32)
                        dst = kq_stack[n * HEAD:(n + 1) * HEAD, kb:qb + 1:qb - kb, h, :].bitcast(F32)
                        sp.dma_start(dst, src).then_inc(kq_stacked[u % 2][h], 16)

            def stack_max(it, u):
                wait_alone(sp, max_split, it * UNITS + u + 1)
                for r, part in ((3 * HEAD, nm_hi), (3 * HEAD + 1, nm_lo)):
                    row = q_stack[r:r + 1, u % 2, :, :].rearrange("p h (t n) -> p (h t) n", n=P)
                    sp.dma_start(row.bitcast(F32), part[:, :].bitcast(F32)).then_inc(max_stacked[u % 2], 16)

            def tiles(rows, c):
                return rows.rearrange("(t p) d -> p t d", p=P)[:, c * CT:(c + 1) * CT, :]

            def load_x(batch):
                for c in range(CHUNKS):
                    sp.dma_start(x[:, c * CT:(c + 1) * CT, :], tiles(x_in[batch], c)).then_inc(x_loaded[c], 16)

            load_x(0)
            for i in range(2):
                load_weights(i, None, attn_w[0])
            load_biases(0)
            for i in range(2, 4):
                load_weights(i, None, attn_w[0])
            with sp.Fori(0, BATCH) as b:
                with sp.Fori(0, LAYERS) as layer:
                    it = b * LAYERS + layer
                    own, other = attn_w[layer], attn_w[1 - layer]
                    load_weights(4, it, own)
                    stack_qk(it, 0)
                    load_weights(5, it, own)
                    load_weights(6, it, own)
                    stack_max(it, 0)
                    load_weights(7, it, own)
                    for u in range(1, UNITS):
                        stack_qk(it, u)
                        stack_max(it, u)
                        if u == UNITS - 2:
                            load_weights(8, it, own)
                    for i in range(9, 12):
                        load_weights(i, it, own)
                    wait_alone(sp, out_bias_added, it * TT + TT)
                    load_biases(1 - layer)
                    for i in range(12, SLOTS + 4):
                        load_weights(i, it, own if i < SLOTS else other)
                for c in range(CHUNKS):
                    wait_alone(sp, rows_drained, (b * LAYERS + LAYERS) * ROWS - (CHUNKS - 1 - c) * CT)
                    sp.dma_start(tiles(out[b], c), x[:, c * CT:(c + 1) * CT, :]).then_inc(x_stored[c], 16)
                for c in range(CHUNKS):
                    wait_alone(sp, x_stored[c], b * 16 + 16)
                    sp.dma_start(x[:, c * CT:(c + 1) * CT, :], tiles(x_in[BATCH - 1], c)).then_inc(x_loaded[c], 16)
            for s in x_loaded:
                sp.wait_ge(s, 16 * (BATCH + 1))
            for s in w_loaded:
                sp.wait_ge(s, 16 * (BATCH * LAYERS * SLOTS + 4) // 2)
            sp.wait_ge(bias_loaded, 48 * (BATCH * LAYERS + 1))

        @block.gpsimd
        def _(pool):
            def split_weights(it, i):
                j = i % SLOTS
                n = it * SLOTS + i
                wait_alone(pool, w_loaded[j % 2], (it * (SLOTS // 2) + i // 2 + 1) * 16)
                before = slot_before(j)
                if before is None and i >= SLOTS:
                    before = max(q for q in range(SLOTS) if place(q) == place(j))
                if before is not None:
                    after = last_product(before)
                    if after[0] == "rows":
                        wait_alone(pool, rows_full, it * ROWS + after[1] + 1)
                    else:
                        wait_alone(pool, ring_full, full(it, after))
                hi, lo, src = w_hi[:, place(j), :], w_lo[:, place(j), :], w_stage[:, j % 2, :]
                pool.tensor_scalar(hi, src, 1.0, 0.0, ALU.mult, ALU.add).then_inc(w_hi_done, 1)
                pool.wait_ge(w_hi_done, n + 1)
                pool.tensor_tensor(lo, src, hi.bitcast(F32), ALU.subtract).then_inc(w_split, 1)

            def last_product(i):
                if i in V_SLOTS:
                    return ("v", TT // 2 - 1)
                if i < WO_SLOT0:
                    return ("proj", (i - QK_SLOT0) * CHUNKS + CHUNKS - 1)
                if i < FFN_SLOT0:
                    return ("rows", TT - 1)
                b, part = divmod(i - FFN_SLOT0, 3)
                x_last = b * CHUNKS + CHUNKS - 1
                return ("rows", TT + x_last * CT + CT - 1) if part == 2 else ("gu", x_last, BT - 1)

            def inverse_deviation(it, ln, c):
                n = it * 2 * CHUNKS + ln * CHUNKS + c + 1
                pool.wait_ge(var_ready, n)
                t = slice(c * CT, (c + 1) * CT)
                pool.tensor_tensor(rstd[:, t], var_eps[:, t], minus_half[:, :], ALU.pow).then_inc(rstd_ready, 1)

            def mask_probs(it, u):
                for d in range(CT):
                    j = key_tiles(u) - CT + d
                    step = J_BASE[u] + j
                    wait_alone(pool, prob_ready, it * S2_STEPS + GH * (step + 1))
                    tile = prob[:, step % 2, :, d * P:(d + 1) * P]
                    pool.affine_select(out=tile, in_=tile, compare_op=ALU.is_ge, fill=0.0, base=0,
                                       pattern=[[0, GH], [1, P]], channel_multiplier=-1).then_inc(mask_done, 1)

            pool.memset(ident[:, :], 0.0).then_inc(const_ready, 1)
            pool.memset(mask_row[:, :], 0.0).then_inc(const_ready, 1)
            pool.memset(minus_half[:, :], -0.5).then_inc(const_ready, 1)
            pool.wait_ge(const_ready, 3)
            pool.affine_select(out=ident[:, :], in_=ident[:, :], compare_op=ALU.not_equal, fill=1.0, base=0,
                               pattern=[[-1, P]], channel_multiplier=1).then_inc(const_ready, 1)
            tri = mask_row[:, TOKENS - P:TOKENS]
            pool.affine_select(out=tri, in_=tri, compare_op=ALU.is_ge, fill=-3e38, base=0,
                               pattern=[[-1, P]], channel_multiplier=1).then_inc(const_ready, 1)
            for i in range(2):
                split_weights(0, i)
            with pool.Fori(0, BATCH * LAYERS) as it:
                inverse_deviation(it, 0, 0)
                split_weights(it, 2)
                inverse_deviation(it, 0, 1)
                for i in range(3, 6):
                    split_weights(it, i)
                pool.wait_ge(xn_ready, it * 2 * TT + TT)
                pool.wait_ge(bias_loaded, it * 48 + 48)
                for t in range(TT):
                    pool.tensor_tensor(x[:, t, :], x[:, t, :], bias_rows[:, 1, :], ALU.add).then_inc(out_bias_added, 1)
                for u in range(UNITS):
                    mask_probs(it, u)
                    if u == 5:
                        split_weights(it, 6)
                    if u == 6:
                        for i in range(7, 11):
                            split_weights(it, i)
                for c in range(CHUNKS):
                    inverse_deviation(it, 1, c)
                for i in range(11, SLOTS + 2):
                    split_weights(it, i)

        @block.scalar
        def _(act):
            with act.Fori(0, BATCH * LAYERS) as it:
                def xt_to_hi(name):
                    r = name[1]
                    act.wait_ge(ring_full, full(it, name))
                    src = buffer_of(name)[:, :, :].rearrange("p t (k n) -> p k t n", n=P)
                    dst = xt_hi[:, :, 2 * r * P:(2 * r + 2) * P].rearrange("p k (t n) -> p k t n", n=P)
                    act.activation(dst, src, ACT.Copy).then_inc(xt_hi_ready, 1)

                def qk_to_hi(u):
                    g, _ = unit(u)
                    act.wait_ge(ring_full, full(it, ("proj", u)))
                    if u == 0:
                        act.wait_ge(bias_loaded, it * 48 + 48)
                    for w in range(2):
                        act.activation(kq_parts[:, 2 - 2 * w, :], buffer_of(("proj", u))[:, w, :], ACT.Identity,
                                       bias=bias_qk[:, w, g:g + 1]).then_inc(qk_hi_ready, 1)

                def exps(u):
                    for j in range(key_tiles(u)):
                        step = J_BASE[u] + j
                        off = max(0, j - CT * unit(u)[1]) * P
                        if step >= 2:
                            act.wait_ge(pv_done, it * KEY_STEPS + step - 1)
                        for h in range(GH):
                            n = GH * step + h
                            act.wait_ge(s2_full, it * S2_STEPS + n + 1)
                            act.activation(prob[:, step % 2, h, off:], bank[n % 2][:, off:], ACT.Exp,
                                           scale=SCALE).then_inc(prob_ready, 1)

                xt_to_hi(("ln1", 0))
                xt_to_hi(("ln1", 1))
                qk_to_hi(0)
                xt_to_hi(("ln1", 2))
                xt_to_hi(("ln1", 3))
                for u in range(UNITS):
                    if u + 1 < UNITS:
                        qk_to_hi(u + 1)
                    exps(u)
                xt_to_hi(("ln2", 0))
                xt_to_hi(("ln2", 1))
                for s in range(STEPS):
                    for t in range(BT):
                        n = s * BT + t
                        act.wait_ge(ring_full, full(it, ("gu", s, t)))
                        if n >= 2:
                            act.wait_ge(ring_drained, drained(it, ("gu", (n - 2) // BT, (n - 2) % BT)))
                        act.activation(silu[:, n % 2, :], buffer_of(("gu", s, t))[:, 0, :], ACT.Silu
                                       ).then_inc(silu_ready, 1)
                    if s == 0:
                        xt_to_hi(("ln2", 2))
                        xt_to_hi(("ln2", 3))

        @block.vector
        def _(dve):
            dve.memset(k_stack[3 * HEAD:3 * HEAD + 2, :, :, :].bitcast(F32), 1.0).then_inc(ring_drained, 1)
            dve.memset(ones[:, :], 1.0).then_inc(ring_drained, 1)
            dve.wait_ge(const_ready, CONSTS)

            def iteration(it, b):
                def tile_stats(t):
                    dve.bn_stats(stats[:, t, :], x[:, t, :]).then_inc(stats_done, 1)

                def chunk_variance(ln, c):
                    n = it * 2 * TT + ln * TT + (c + 1) * CT
                    wait_alone(dve, stats_done, 2 * n - CT)
                    for t in range(c * CT, (c + 1) * CT):
                        dve.bn_aggr(mean_var[:, t, :], stats[:, t, :]).then_inc(stats_done, 1)
                    dve.wait_ge(stats_done, 2 * n)
                    t = slice(c * CT, (c + 1) * CT)
                    dve.tensor_scalar(var_eps[:, t], mean_var[:, t, 1], EPS, None, ALU.add).then_inc(var_ready, 1)

                def normalise_pair(ln, r):
                    if r:
                        dve.wait_ge(ring_full, full(it, (f"ln{ln + 1}", r - 1)))
                    dve.wait_ge(rstd_ready, it * 2 * CHUNKS + ln * CHUNKS + 2 * r // CT + 1)
                    for t in (2 * r, 2 * r + 1):
                        dve.tensor_scalar(xn[:, t % 2, :], x[:, t, :], mean_var[:, t, 0:1], rstd[:, t:t + 1],
                                          ALU.subtract, ALU.mult).then_inc(xn_ready, 1)

                def xt_to_lo(ln, r):
                    name = (f"ln{ln + 1}", r)
                    dve.wait_ge(xt_hi_ready, it * TT + ln * (TT // 2) + r + 1)
                    for t in range(2):
                        cols = slice((2 * r + t) * P, (2 * r + t + 1) * P)
                        src = buffer_of(name)[:, t, :].rearrange("p (k n) -> p k n", n=P)
                        ins = dve.tensor_tensor(xt_lo[:, :, cols], src, xt_hi[:, :, cols].bitcast(F32), ALU.subtract)
                    ins.then_inc(ring_drained, 1)

                def take_v(r):
                    dve.wait_ge(ring_full, full(it, ("v", r)))
                    for t in range(2):
                        ins = dve.tensor_tensor(v[:, 2 * r + t, :], buffer_of(("v", r))[:, t, :], bias_rows[:, 0, :],
                                                ALU.add)
                    ins.then_inc(ring_drained, 1)

                def qk_to_lo(u):
                    g, _ = unit(u)
                    for w in range(2):
                        dve.wait_ge(qk_hi_ready, it * 2 * UNITS + 2 * u + w + 1)
                        part = 2 - 2 * w
                        ins = dve.scalar_tensor_tensor(kq_parts[:, part + 1, :], buffer_of(("proj", u))[:, w, :],
                                                       bias_qk[:, w, g:g + 1], kq_parts[:, part, :].bitcast(F32),
                                                       ALU.add, ALU.subtract)
                    ins.then_inc(ring_drained, 1)

                def maxima(u):
                    _, c = unit(u)
                    for s in range(GH * CT):
                        keys = (c * CT + s % CT + 1) * P
                        src = buffer_of(("s1", u, s))[:, :, :].rearrange("p b n -> p (b n)")
                        wait_alone(dve, ring_full, full(it, ("s1", u, s)))
                        ins = dve.tensor_tensor_reduce(
                            out=sum_out[:, s % 2, 0:keys], in0=src[:, 0:keys], in1=mask_row[:, TOKENS - keys:],
                            scale=1.0, scalar=-3.3e38, op0=ALU.add, op1=ALU.max,
                            accum_out=row_max[:, u % 2, s:s + 1])
                        ins.then_inc(ring_drained, 1)
                    dve.wait_ge(ring_full, full(it, ("mt", u)))
                    src = buffer_of(("mt", u))[0:GH * CT, 0, 0:P]
                    if u:
                        dve.wait_ge(max_stacked[(u - 1) % 2], stacked(it, u - 1, 2))
                    dve.tensor_scalar(nm_hi[:, :], src, -1.0, None, ALU.mult).then_inc(nm_hi_done, 1)
                    dve.wait_ge(nm_hi_done, it * UNITS + u + 1)
                    dve.scalar_tensor_tensor(nm_lo[:, :], src, -1.0, nm_hi[:, :].bitcast(F32), ALU.mult,
                                             ALU.subtract).then_inc(max_split, 1)
                    dve.wait_ge(max_split, it * UNITS + u + 1)
                    dve.tensor_copy(row_max[0:1, u % 2, 0:1], row_max[0:1, u % 2, 0:1]).then_inc(ring_drained, 1)

                def normalise_attn(u):
                    g, c = unit(u)
                    dve.wait_ge(pv_done, it * KEY_STEPS + J_BASE[u] + key_tiles(u))
                    if u:
                        dve.wait_ge(attn_ready, it * UNITS + u)
                    dve.reciprocal(recip[:, :], den_bank[:, :]).then_inc(recip_done, 1)
                    dve.wait_ge(recip_done, it * UNITS + u + 1)
                    dve.tensor_tensor(attn[:, g, c * CHUNK:(c + 1) * CHUNK], out_bank[:, :], recip[:, :], ALU.mult
                                      ).then_inc(attn_ready, 1)

                def split_attn(u):
                    g, c = unit(u)
                    cols = slice(c * CHUNK, (c + 1) * CHUNK)
                    dve.wait_ge(attn_ready, it * UNITS + u + 1)
                    dve.tensor_copy(xt_hi[:, g, cols], attn[:, g, cols]).then_inc(attn_hi_done, 1)
                    dve.wait_ge(attn_hi_done, it * UNITS + u + 1)
                    dve.tensor_tensor(xt_lo[:, g, cols], attn[:, g, cols], xt_hi[:, g, cols].bitcast(F32),
                                      ALU.subtract).then_inc(attn_split, 1)

                def add_rows(row, t, b):
                    dve.wait_ge(rows_full, it * ROWS + row + 1)
                    dve.tensor_tensor(x[:, t, :], x[:, t, :], bank[b][:, :], ALU.add).then_inc(rows_drained, 1)

                def hidden_parts(s, t):
                    n = s * BT + t
                    dve.wait_ge(silu_ready, it * HID_TILES + n + 1)
                    if n >= 2:
                        dve.wait_ge(h_ready, it * HID_TILES + n - 1)
                    dve.tensor_tensor(hidden[:, n % 2, :], silu[:, n % 2, :], buffer_of(("gu", s, t))[:, 1, :], ALU.mult
                                      ).then_inc(ring_drained, 1)
                    dve.wait_ge(ring_drained, drained(it, ("gu", s, t)))
                    hi = h_parts[:, s % 2, 0, t, :]
                    dve.tensor_copy(hi, hidden[:, n % 2, :]).then_inc(h_hi_done, 1)
                    dve.wait_ge(h_hi_done, it * HID_TILES + n + 1)
                    dve.tensor_tensor(h_parts[:, s % 2, 1, t, :], hidden[:, n % 2, :], hi.bitcast(F32), ALU.subtract
                                      ).then_inc(h_ready, 1)

                def down_rows(s):
                    for t in range(CT):
                        add_rows(TT + s * CT + t, s % CHUNKS * CT + t, t)

                def chunk_stats(c):
                    dve.wait_ge(x_loaded[c], b * 16 + 16)
                    for t in range(c * CT, (c + 1) * CT):
                        tile_stats(t)
                    chunk_variance(0, c)

                chunk_stats(0)
                normalise_pair(0, 0)
                normalise_pair(0, 1)
                xt_to_lo(0, 0)
                xt_to_lo(0, 1)
                chunk_stats(1)
                normalise_pair(0, 2)
                dve.wait_ge(bias_loaded, it * 48 + 48)
                take_v(0)
                take_v(1)
                qk_to_lo(0)
                normalise_pair(0, 3)
                xt_to_lo(0, 2)
                xt_to_lo(0, 3)
                take_v(2)
                take_v(3)
                maxima(0)
                for u in range(UNITS):
                    if u + 1 < UNITS:
                        qk_to_lo(u + 1)
                    if u:
                        normalise_attn(u - 1)
                    if u + 1 < UNITS:
                        maxima(u + 1)
                for u in range(UNITS - 1):
                    split_attn(u)
                normalise_attn(UNITS - 1)
                split_attn(UNITS - 1)
                dve.wait_ge(out_bias_added, it * TT + TT)
                for c in range(CHUNKS):
                    for t in range(c * CT, (c + 1) * CT):
                        add_rows(t, t, t % 2)
                        dve.wait_ge(rows_drained, it * ROWS + t + 1)
                        tile_stats(t)
                    chunk_variance(1, c)
                normalise_pair(1, 0)
                normalise_pair(1, 1)
                xt_to_lo(1, 0)
                xt_to_lo(1, 1)
                normalise_pair(1, 2)
                for s in range(STEPS):
                    for t in range(BT):
                        hidden_parts(s, t)
                    if s == 0:
                        normalise_pair(1, 3)
                        xt_to_lo(1, 2)
                        xt_to_lo(1, 3)
                    for d in downs_after(s):
                        down_rows(d)

            with dve.Fori(0, BATCH) as b:
                with dve.Fori(0, LAYERS) as layer:
                    iteration(b * LAYERS + layer, b)

        @block.tensor
        def _(pe):
            pe.wait_ge(const_ready, CONSTS)
            pe.wait_ge(ring_drained, RING_CREDIT)

            def iteration(it):
                def three(dst, terms, last_inc=None):
                    n = len(terms)
                    for k, (ah, al, bh, bl) in enumerate(terms):
                        pe.matmul(dst, ah, bh, start=k == 0, stop=False)
                        pe.matmul(dst, ah, bl, start=False, stop=False)
                        ins = pe.matmul(dst, al, bh, start=False, stop=k == n - 1)
                    return ins

                def w_part(slot, cols):
                    i = place(slot)
                    return w_hi[:, i, cols], w_lo[:, i, cols]

                def xt_part(k, cols):
                    return xt_hi[:, k, cols], xt_lo[:, k, cols]

                def transpose_pair(ln, r):
                    name = (f"ln{ln + 1}", r)
                    pe.wait_ge(ring_drained, buffer_free(it, name))
                    pe.wait_ge(xn_ready, it * 2 * TT + ln * TT + 2 * r + 2)
                    for t in range(2):
                        for k in range(KT):
                            ins = pe.transpose(buffer_of(name)[:, t, k * P:(k + 1) * P], xn[:, t, k * P:(k + 1) * P],
                                               ident[:, :])
                    ins.then_inc(ring_full, 1)

                def v_pair(r):
                    pe.wait_ge(ring_drained, buffer_free(it, ("v", r)))
                    pe.wait_ge(ring_drained, drained(it, ("ln1", r)))
                    pe.wait_ge(w_split, it * SLOTS + V_SLOTS[1] + 1)
                    for t in range(2):
                        cols = slice((2 * r + t) * P, (2 * r + t + 1) * P)
                        terms = [(*xt_part(k, cols), *w_part(V_SLOTS[k // 2], slice(k % 2 * DIM, (k % 2 + 1) * DIM)))
                                 for k in range(KT)]
                        ins = three(buffer_of(("v", r))[:, t, :], terms)
                    ins.then_inc(ring_full, 1)

                def project_qk(u):
                    g, c = unit(u)
                    pe.wait_ge(ring_drained, buffer_free(it, ("proj", u)))
                    pe.wait_ge(ring_drained, drained(it, ("ln1", 2 * c + 1)))
                    pe.wait_ge(w_split, it * SLOTS + QK_SLOT0 + g + 1)
                    cols = slice(c * CHUNK, (c + 1) * CHUNK)
                    for w in range(2):
                        terms = [(*w_part(QK_SLOT0 + g, slice((2 * k + w) * P, (2 * k + w + 1) * P)), *xt_part(k, cols))
                                 for k in range(KT)]
                        ins = three(buffer_of(("proj", u))[:, w, :], terms)
                    ins.then_inc(ring_full, 1)

                def keys_of(u, chunk):
                    return (u - unit(u)[1] + chunk) % 3

                def scores(u, s):
                    _, c = unit(u)
                    h, t = divmod(s, CT)
                    if t == 0:
                        pe.wait_ge(kq_stacked[u % 2][h], stacked(it, u, len(STACKED)))
                    pe.wait_ge(ring_drained, buffer_free(it, ("s1", u, s)))
                    q = q_stack[0:3 * HEAD, u % 2, h, t * P:(t + 1) * P]
                    for kc in range(c + 1):
                        n = CHUNK if kc < c else (t + 1) * P
                        ins = pe.matmul(buffer_of(("s1", u, s))[:, kc, 0:n], q,
                                        k_stack[0:3 * HEAD, keys_of(u, kc), h, 0:n], start=True, stop=True)
                    ins.then_inc(ring_full, 1)

                def transpose_max(u):
                    pe.wait_ge(ring_drained, buffer_free(it, ("mt", u)))
                    pe.wait_ge(ring_drained, drained(it, ("s1", u, GH * CT - 1)))
                    pe.transpose(buffer_of(("mt", u))[0:GH * CT, 0, 0:P], row_max[:, u % 2, :], ident[:, :]
                                 ).then_inc(ring_full, 1)

                def scores_t(u, j, h):
                    _, c = unit(u)
                    n = GH * (J_BASE[u] + j) + h
                    off = max(0, j - CT * c) * P
                    if j == 0 and h == 0:
                        pe.wait_ge(max_stacked[u % 2], stacked(it, u, 2))
                    if n >= 2:
                        pe.wait_ge(prob_ready, it * S2_STEPS + n - 1)
                    rows = slice(0, 3 * HEAD + 2)
                    pe.matmul(bank[n % 2][:, off:], k_stack[rows, keys_of(u, j // CT), h, j % CT * P:(j % CT + 1) * P],
                              q_stack[rows, u % 2, h, off:], start=True, stop=True).then_inc(s2_full, 1)

                def weigh_values(u, j):
                    g, c = unit(u)
                    step = J_BASE[u] + j
                    last = j == key_tiles(u) - 1
                    d = j - CT * c
                    off = max(0, d) * P
                    pe.wait_ge(prob_ready, it * S2_STEPS + GH * (step + 1))
                    if d >= 0:
                        pe.wait_ge(mask_done, it * UNITS * CT + u * CT + d + 1)
                    if j == 0 and u:
                        pe.wait_ge(attn_ready, it * UNITS + u)
                    for dst, src in ((out_bank, None), (den_bank, ones)):
                        for h in range(GH):
                            rows = slice(h * HEAD, (h + 1) * HEAD)
                            a = v[:, j, g * P + h * HEAD:g * P + (h + 1) * HEAD] if src is None else src[:, :]
                            ins = pe.matmul(dst[rows, off:], a, prob[:, step % 2, h, off:], start=j == 0, stop=last,
                                            tile_position=(0, h * HEAD))
                    ins.then_inc(pv_done, 1)

                def project_out(t):
                    if t >= 2:
                        pe.wait_ge(rows_drained, it * ROWS + t - 1)
                    if t % CT == 0:
                        pe.wait_ge(attn_split, it * UNITS + (UNITS - 1 if t < CT else UNITS))
                        pe.wait_ge(w_split, it * SLOTS + WO_SLOT0 + 2)
                    cols = slice(t * P, (t + 1) * P)
                    terms = [(*xt_part(g, cols), *w_part(WO_SLOT0 + g // 2, slice(g % 2 * DIM, (g % 2 + 1) * DIM)))
                             for g in range(GROUPS)]
                    three(bank[t % 2][:, :], terms).then_inc(rows_full, 1)

                def gate_up(s):
                    b, c = divmod(s, CHUNKS)
                    cols = slice(c * CHUNK, (c + 1) * CHUNK)
                    if b == 0:
                        pe.wait_ge(ring_drained, drained(it, ("ln2", 2 * c + 1)))
                    if c == 0:
                        pe.wait_ge(w_split, it * SLOTS + FFN_SLOT0 + 3 * b + 2)
                    for t in range(BT):
                        pe.wait_ge(ring_drained, buffer_free(it, ("gu", s, t)))
                        for w in range(2):
                            terms = [(*w_part(FFN_SLOT0 + 3 * b + w, slice(k * BLOCK + t * P, k * BLOCK + (t + 1) * P)),
                                      *xt_part(k, cols)) for k in range(KT)]
                            ins = three(buffer_of(("gu", s, t))[:, w, :], terms)
                        ins.then_inc(ring_full, 1)

                def down(s):
                    b, c = divmod(s, CHUNKS)
                    pe.wait_ge(h_ready, it * HID_TILES + (s + 1) * BT)
                    if c == 0:
                        pe.wait_ge(w_split, it * SLOTS + FFN_SLOT0 + 3 * b + 3)
                    for t in range(CT):
                        row = TT + s * CT + t
                        pe.wait_ge(rows_drained, it * ROWS + (TT if s == 0 else row - CT + 1))
                        tok = slice(t * P, (t + 1) * P)
                        terms = [(h_parts[:, s % 2, 0, i, tok], h_parts[:, s % 2, 1, i, tok],
                                  *w_part(FFN_SLOT0 + 3 * b + 2, slice(i * DIM, (i + 1) * DIM))) for i in range(BT)]
                        three(bank[t][:, :], terms).then_inc(rows_full, 1)

                transpose_pair(0, 0)
                transpose_pair(0, 1)
                v_pair(0)
                v_pair(1)
                project_qk(0)
                transpose_pair(0, 2)
                transpose_pair(0, 3)
                v_pair(2)
                v_pair(3)
                for s in range(GH * CT):
                    scores(0, s)
                transpose_max(0)
                LEAD = 2 * GH
                for u in range(UNITS):
                    if u + 1 < UNITS:
                        project_qk(u + 1)
                    if u:
                        weigh_values(u - 1, key_tiles(u - 1) - 1)
                    steps = [(j, h) for j in range(key_tiles(u)) for h in range(GH)]
                    done = 0
                    for n, (j, h) in enumerate(steps):
                        scores_t(u, j, h)
                        if h == GH - 1 and j:
                            weigh_values(u, j - 1)
                        if u + 1 < UNITS and n + 1 >= LEAD:
                            upto = (n + 1 - LEAD) * GH * CT // (len(steps) - LEAD)
                            for s in range(done, upto):
                                scores(u + 1, s)
                            done = upto
                    if u + 1 < UNITS:
                        transpose_max(u + 1)
                weigh_values(UNITS - 1, key_tiles(UNITS - 1) - 1)
                for t in range(TT):
                    project_out(t)
                transpose_pair(1, 0)
                transpose_pair(1, 1)
                for s in range(STEPS):
                    gate_up(s)
                    if s == 0:
                        transpose_pair(1, 2)
                        transpose_pair(1, 3)
                    for d in downs_after(s):
                        down(d)

            with pe.Fori(0, BATCH * LAYERS) as it:
                iteration(it)


def lay_out(np, L0_attn_a_x, L0_attn_a_W_qkv, L0_attn_a_b_qkv, L0_attn_a_W_out, L0_attn_a_b_out, L0_attn_b_w_qkv,
            L0_attn_b_b_qkv, L0_attn_b_w_proj, L0_attn_b_b_proj, L0_ffn_w_gate, L0_ffn_w_up, L0_ffn_w_down):
    def row_pairs(w):
        return np.asarray(w).reshape(2, 2, P, DIM).transpose(0, 2, 1, 3).reshape(2, P, SLOT)

    def attn_slots(qkv, proj):
        q, k = (qkv[:, n * DIM:(n + 1) * DIM].reshape(KT, P, GROUPS, 1, P) for n in range(2))
        qk = np.concatenate([q, k], 3).transpose(2, 1, 0, 3, 4).reshape(GROUPS, P, SLOT)
        return np.concatenate([row_pairs(qkv[:, 2 * DIM:]), qk, row_pairs(proj)])

    def column_blocks(w):
        return w.reshape(KT, P, BLOCKS, BLOCK).transpose(2, 1, 0, 3).reshape(BLOCKS, 1, P, SLOT)

    down = L0_ffn_w_down.T.reshape(BLOCKS, 1, BT, P, DIM).transpose(0, 1, 3, 2, 4).reshape(BLOCKS, 1, P, SLOT)
    ffn = np.concatenate([column_blocks(L0_ffn_w_gate.T), column_blocks(L0_ffn_w_up.T), down], 1)
    qkv_biases = (L0_attn_a_b_qkv, L0_attn_b_b_qkv)
    return {
        "x_in": L0_attn_a_x,
        "attn_w": np.stack([attn_slots(L0_attn_a_W_qkv.T, L0_attn_a_W_out.T),
                            attn_slots(L0_attn_b_w_qkv, L0_attn_b_w_proj)]),
        "ffn_w": ffn.reshape(3 * BLOCKS, P, SLOT),
        "qk_bias": np.stack([b[:2 * DIM].reshape(2, GROUPS, P).transpose(2, 0, 1) for b in qkv_biases]),
        "row_bias": np.stack([np.stack([b[2 * DIM:], o])
                              for b, o in zip(qkv_biases, (L0_attn_a_b_out, L0_attn_b_b_proj))]),
    }


def kernel(**inputs):
    import numpy as np
    import concourse.bacc as bacc
    from concourse.bass_utils import run_bass_kernel_spmd

    nc = bacc.Bacc("TRN2", target_bir_lowering=False, num_devices=1)
    laid = {n: np.ascontiguousarray(a) for n, a in lay_out(np, **{n: np.asarray(a) for n, a in inputs.items()}).items()}
    args = [nc.dram_tensor(n, a.shape, mybir.dt.from_np(a.dtype), kind="ExternalInput").ap() for n, a in laid.items()]
    out = nc.dram_tensor("out", (BATCH, TOKENS, DIM), F32, kind="ExternalOutput").ap()
    block_kernel(nc, *args, out)
    r = run_bass_kernel_spmd(nc, [laid], core_ids=[0])
    return r.results[0]["out"]
```

```python
from contextlib import ExitStack

import concourse.bass as bass
from concourse import mybir

F32 = mybir.dt.float32
F32R = mybir.dt.float32r
BF16 = mybir.dt.bfloat16
ALU = mybir.AluOpType
ACT = mybir.ActivationFunctionType

P = 128
BATCH, TOKENS, DIM, HIDDEN, HEADS = 2, 1024, 512, 2048, 16
LAYERS = 2
HEAD = DIM // HEADS
SCALE = float(HEAD) ** -0.5
EPS = 1e-5
KT = DIM // P
TT = TOKENS // P
CHUNK = 512
CT = CHUNK // P
CHUNKS = TOKENS // CHUNK
GH = P // HEAD
GROUPS = HEADS // GH
UNITS = GROUPS * CHUNKS
BLOCK = 256
BT = BLOCK // P
BLOCKS = HIDDEN // BLOCK
STEPS = BLOCKS * CHUNKS

SLOT = 1024
V_SLOTS, QK_SLOT0, WO_SLOT0, FFN_SLOT0 = (0, 1), 2, 2 + GROUPS, 4 + GROUPS
SLOTS = FFN_SLOT0 + 3 * BLOCKS
SPLIT_BESIDE = {1: (WO_SLOT0,), 4: (WO_SLOT0 + 1,), 5: (FFN_SLOT0,), 7: (FFN_SLOT0 + 1, FFN_SLOT0 + 2)}
LOAD_BESIDE = {3: FFN_SLOT0, 5: FFN_SLOT0 + 1, 6: FFN_SLOT0 + 2}
PLACES = 5
LENT_PLACES = (0, 1)
ATTN_PLACES = (*LENT_PLACES, 2, 3, 4, 2, 3, 4)
FFN_PLACES = (2, 0, 1, 3, 4)


def place(i):
    return ATTN_PLACES[i] if i < FFN_SLOT0 else FFN_PLACES[(i - FFN_SLOT0) % PLACES]


def slot_before(i):
    return max((j for j in range(i) if place(j) == place(i)), default=None)


def unit(u):
    return u // CHUNKS, u % CHUNKS


def key_tiles(u):
    return CT * (unit(u)[1] + 1)


def downs_after(s):
    return {0: (), STEPS - 2: (s - 1, s), STEPS - 1: (s,)}.get(s, (s - 1,))


def beside(u):
    def s1(w):
        first = EARLY if w < UNITS and unit(w)[1] else 0
        return [("s1", w, s) for s in range(GH * CT)], first

    if u + 1 >= UNITS:
        return []
    tiles, first = s1(u + 1)
    if u < 0:
        own = []
        for n in range(CT):
            own += [("v", CT + n), *tiles[n * GH:(n + 1) * GH]]
        own.append(("mt", 0))
        return own + s1(1)[0][:EARLY]
    own = tiles[first:] + [("mt", u + 1)]
    if u + 2 < UNITS and unit(u + 2)[1]:
        ahead = s1(u + 2)[0][:EARLY]
        own = own[:-1] + ahead[:1] + own[-1:] + ahead[1:]
    return own


def ring_order():
    yield from (("ln1", 0), ("ln1", 1), *(("v", t) for t in range(CT)), ("proj", 0))
    yield from (("ln1", 2), ("ln1", 3), ("proj", 1))
    for u in range(-1, UNITS):
        if 0 <= u < UNITS - 2:
            yield ("proj", u + 2)
        yield from beside(u)
    yield from (("ln2", 0), ("ln2", 1))
    for x in range(STEPS):
        yield from (("gu", x, t) for t in range(BT))
        if x == 0:
            yield from (("ln2", 2), ("ln2", 3))


TAIL = 3
EARLY = 5
RING = {name: n for n, name in enumerate(ring_order())}
RING_USES = len(RING)
assert RING_USES % 2 == 0 and SLOTS % 2 == 0
J_BASE = [sum(key_tiles(v) for v in range(u)) for u in range(UNITS)]
KEY_STEPS = sum(key_tiles(u) for u in range(UNITS))
S2_STEPS = GH * KEY_STEPS
ROWS = TT + STEPS * CT
HID_TILES = STEPS * BT
K_BUFS, Q_BUFS = 4, 3
PLACE_AT = (0, *range(K_BUFS + Q_BUFS - 1, K_BUFS + Q_BUFS + PLACES - len(LENT_PLACES)))
STACKED = ((0, 2), (0, 3), (1, 2))


def block_kernel(nc, x_in, attn_w, ffn_w, qk_bias, row_bias, out):
    with ExitStack() as ctx:
        def sb(name, shape, dt=F32):
            return ctx.enter_context(nc.sbuf_tensor(name, shape, dt))

        def sem(name):
            return ctx.enter_context(nc.semaphore(name))

        x = sb("x", [P, TT, DIM])
        xt_hi = sb("xt_hi", [P, KT, TOKENS], F32R)
        xt_lo = sb("xt_lo", [P, KT, TOKENS], F32R)
        v = sb("v", [P, TT, DIM])
        attn = sb("attn", [P, GROUPS, TOKENS])
        area = sb("area", [P, K_BUFS + Q_BUFS + PLACES - len(LENT_PLACES), 2 * SLOT], F32R)
        kq_stack = area[:, 0:K_BUFS + Q_BUFS, :].rearrange("p b (h n) -> p b h n", h=GH)
        k_stack = kq_stack[:, 0:K_BUFS, :, :]
        q_stack = kq_stack[:, K_BUFS:, :, :]
        h_parts = q_stack[:, 0:2, :, :].rearrange("p b (s t) n -> p b s t n", s=2)
        prob = sb("prob", [P, 2, GH, CHUNK])
        silu = prob[:, 0, 0:2, :]
        hidden = prob[:, 1, 0:2, :]
        kq_parts = sb("kq_parts", [P, 4, CHUNK], F32R)
        mask_row = sb("mask_row", [P, TOKENS], BF16)
        xn = sb("xn", [P, 2, DIM])
        sum_out = xn[:, :, :].bitcast(BF16)
        w_stage = sb("w_stage", [P, 2, SLOT])
        recip = sb("recip", [P, CHUNK])
        bias_rows = sb("bias_rows", [P, 2, DIM])
        bias_qk = sb("bias_qk", [P, 2, GROUPS])
        ident = sb("ident", [P, P])
        ones = sb("ones", [P, HEAD])
        row_max = sb("row_max", [P, 2, GH * CT])
        nm_hi = sb("nm_hi", [GH * CT, P], F32R)
        nm_lo = sb("nm_lo", [GH * CT, P], F32R)
        stats = sb("stats", [P, TT, 6])
        mean_var = sb("mean_var", [P, TT, 2])
        var_eps = sb("var_eps", [P, TT])
        rstd = sb("rstd", [P, TT])
        minus_half = sb("minus_half", [P, CT])

        ring = [ctx.enter_context(nc.psum_tensor(f"ring{i}", [P, 2, CHUNK], F32)) for i in range(2)]
        bank = [ctx.enter_context(nc.psum_tensor(f"bank{i}", [P, CHUNK], F32)) for i in range(4)]
        out_bank, den_bank = bank[2], bank[3]

        x_loaded, x_stored = ([sem(f"x_{what}{c}") for c in range(CHUNKS)] for what in ("loaded", "stored"))
        bias_loaded = sem("bias_loaded")
        w_loaded = [sem("w_loaded0"), sem("w_loaded1")]
        kq_stacked = [[sem(f"kq_stacked{n}_{h}") for h in range(GH)] for n in range(2)]
        max_stacked = [sem("max_stacked0"), sem("max_stacked1")]
        const_ready, w_split, w_hi_done = sem("const_ready"), sem("w_split"), sem("w_hi_done")
        rstd_ready, out_bias_added, mask_done = sem("rstd_ready"), sem("out_bias_added"), sem("mask_done")
        ones_ready = sem("ones_ready")
        ring_full, s2_full, pv_done, rows_full = sem("ring_full"), sem("s2_full"), sem("pv_done"), sem("rows_full")
        xt_hi_ready, qk_hi_ready, prob_ready, silu_ready = (
            sem("xt_hi_ready"), sem("qk_hi_ready"), sem("prob_ready"), sem("silu_ready"))
        ring_drained, stats_done, var_ready, xn_ready = (
            sem("ring_drained"), sem("stats_done"), sem("var_ready"), sem("xn_ready"))
        max_ready, nm_hi_done, max_split, recip_done = (
            sem("max_ready"), sem("nm_hi_done"), sem("max_split"), sem("recip_done"))
        attn_ready, attn_hi_done, attn_split = sem("attn_ready"), sem("attn_hi_done"), sem("attn_split")
        h_hi_done, h_ready, rows_drained = sem("h_hi_done"), sem("h_ready"), sem("rows_drained")

        RING_CREDIT = 2

        def k_buffer(u):
            return (u - 2) % K_BUFS

        def q_buffer(u):
            return u % Q_BUFS

        def buffer_of(name):
            return ring[RING[name] % 2]

        def full(it, name):
            return it * RING_USES + RING[name] + 1

        def drained(it, name):
            return it * RING_USES + RING[name] + 1 + RING_CREDIT

        def buffer_free(it, name):
            return it * RING_USES + RING[name] - 1 + RING_CREDIT

        def stacked(it, u, each):
            return 16 * each * (it * (UNITS // 2) + u // 2 + 1)

        def w_part(slot, cols):
            at = PLACE_AT[place(slot)]
            return area[:, at, cols], area[:, at, cols.start + SLOT:cols.stop + SLOT]

        CONSTS = 5

        def wait_alone(eng, semaphore, value):
            if not isinstance(value, int):
                value = eng.snap(eng.to_reg(value))
            eng.wait_ge(const_ready, CONSTS)
            eng.wait_ge(semaphore, value)

        block = ctx.enter_context(nc.Block())

        @block.sync
        def _(sp):
            def load_weights(i, it, attn_src):
                if i >= 2 or it is not None:
                    wait_alone(sp, w_split, (0 if it is None else it * SLOTS) + i - 1)
                j = i % SLOTS
                src = attn_src[j] if j < FFN_SLOT0 else ffn_w[j - FFN_SLOT0]
                sp.dma_start(w_stage[:, j % 2, :], src).then_inc(w_loaded[j % 2], 16)

            def load_biases(layer):
                sp.dma_start(bias_qk[:, :, :], qk_bias[layer]).then_inc(bias_loaded, 16)
                for r in range(2):
                    sp.dma_start(bias_rows[:, r, :], row_bias[layer, r:r + 1, :].to_broadcast([P, DIM])
                                 ).then_inc(bias_loaded, 16)

            def stack_qk(it, u):
                wait_alone(sp, ring_drained, drained(it, ("proj", u)))
                kb, qb = k_buffer(u), K_BUFS + q_buffer(u)
                for h in range(GH):
                    rows = slice(h * HEAD, (h + 1) * HEAD)
                    for n, (k, q) in enumerate(STACKED):
                        src = kq_parts[rows, k:q + 1:q - k, :].bitcast(F32)
                        dst = kq_stack[n * HEAD:(n + 1) * HEAD, kb:qb + 1:qb - kb, h, :].bitcast(F32)
                        sp.dma_start(dst, src).then_inc(kq_stacked[u % 2][h], 16)

            def stack_max(it, u):
                wait_alone(sp, max_split, it * UNITS + u + 1)
                for r, part in ((3 * HEAD, nm_hi), (3 * HEAD + 1, nm_lo)):
                    row = q_stack[r:r + 1, q_buffer(u), :, :].rearrange("p h (t n) -> p (h t) n", n=P)
                    sp.dma_start(row.bitcast(F32), part[:, :].bitcast(F32)).then_inc(max_stacked[u % 2], 16)

            def tiles(rows, c):
                return rows.rearrange("(t p) d -> p t d", p=P)[:, c * CT:(c + 1) * CT, :]

            def load_x(batch):
                for c in range(CHUNKS):
                    sp.dma_start(x[:, c * CT:(c + 1) * CT, :], tiles(x_in[batch], c)).then_inc(x_loaded[c], 16)

            load_x(0)
            for i in range(2):
                load_weights(i, None, attn_w[0])
            load_biases(0)
            for i in range(2, 4):
                load_weights(i, None, attn_w[0])
            with sp.Fori(0, BATCH) as b:
                with sp.Fori(0, LAYERS) as layer:
                    it = b * LAYERS + layer
                    own, other = attn_w[layer], attn_w[1 - layer]
                    load_weights(4, it, own)
                    stack_qk(it, 0)
                    load_weights(5, it, own)
                    load_weights(6, it, own)
                    stack_qk(it, 1)
                    stack_max(it, 0)
                    load_weights(7, it, own)
                    for u in range(UNITS - 1):
                        if u + 2 < UNITS:
                            stack_qk(it, u + 2)
                        stack_max(it, u + 1)
                        if u in LOAD_BESIDE:
                            load_weights(LOAD_BESIDE[u], it, own)
                    for i in range(11, 12):
                        load_weights(i, it, own)
                    wait_alone(sp, out_bias_added, it * TT + TT)
                    load_biases(1 - layer)
                    for i in range(12, SLOTS + 4):
                        load_weights(i, it, own if i < SLOTS else other)
                for c in range(CHUNKS):
                    wait_alone(sp, rows_drained, (b * LAYERS + LAYERS) * ROWS - (CHUNKS - 1 - c) * CT)
                    sp.dma_start(tiles(out[b], c), x[:, c * CT:(c + 1) * CT, :]).then_inc(x_stored[c], 16)
                for c in range(CHUNKS):
                    wait_alone(sp, x_stored[c], b * 16 + 16)
                    sp.dma_start(x[:, c * CT:(c + 1) * CT, :], tiles(x_in[BATCH - 1], c)).then_inc(x_loaded[c], 16)
            for s in x_loaded:
                sp.wait_ge(s, 16 * (BATCH + 1))
            for s in w_loaded:
                sp.wait_ge(s, 16 * (BATCH * LAYERS * SLOTS + 4) // 2)
            sp.wait_ge(bias_loaded, 48 * (BATCH * LAYERS + 1))

        @block.gpsimd
        def _(pool):
            def split_weights(it, i):
                j = i % SLOTS
                n = it * SLOTS + i
                wait_alone(pool, w_loaded[j % 2], (it * (SLOTS // 2) + i // 2 + 1) * 16)
                before = slot_before(j)
                if before is None and i >= SLOTS:
                    before = max(q for q in range(SLOTS) if place(q) == place(j))
                if before is not None:
                    after = last_product(before)
                    if after[0] == "rows":
                        wait_alone(pool, rows_full, it * ROWS + after[1] + 1)
                    else:
                        wait_alone(pool, ring_full, full(it, after))
                if j >= FFN_SLOT0 and place(j) in LENT_PLACES and slot_before(j) in V_SLOTS:
                    wait_alone(pool, s2_full, it * S2_STEPS + S2_STEPS)
                hi, lo, src = *w_part(j, slice(0, SLOT)), w_stage[:, j % 2, :]
                pool.tensor_scalar(hi, src, 1.0, 0.0, ALU.mult, ALU.add).then_inc(w_hi_done, 1)
                pool.wait_ge(w_hi_done, n + 1)
                pool.tensor_tensor(lo, src, hi.bitcast(F32), ALU.subtract).then_inc(w_split, 1)

            def last_product(i):
                if i in V_SLOTS:
                    return ("v", TT - 1)
                if i < WO_SLOT0:
                    return ("proj", (i - QK_SLOT0) * CHUNKS + CHUNKS - 1)
                if i < FFN_SLOT0:
                    return ("rows", TT - 1)
                b, part = divmod(i - FFN_SLOT0, 3)
                x_last = b * CHUNKS + CHUNKS - 1
                return ("rows", TT + x_last * CT + CT - 1) if part == 2 else ("gu", x_last, BT - 1)

            def inverse_deviation(it, ln, c):
                n = it * 2 * CHUNKS + ln * CHUNKS + c + 1
                pool.wait_ge(var_ready, n)
                t = slice(c * CT, (c + 1) * CT)
                pool.tensor_tensor(rstd[:, t], var_eps[:, t], minus_half[:, :], ALU.pow).then_inc(rstd_ready, 1)

            def mask_probs(it, u):
                for d in range(CT):
                    j = key_tiles(u) - CT + d
                    step = J_BASE[u] + j
                    wait_alone(pool, prob_ready, it * S2_STEPS + GH * (step + 1))
                    tile = prob[:, step % 2, :, d * P:(d + 1) * P]
                    pool.affine_select(out=tile, in_=tile, compare_op=ALU.is_ge, fill=0.0, base=0,
                                       pattern=[[0, GH], [1, P]], channel_multiplier=-1).then_inc(mask_done, 1)

            pool.memset(ident[:, :], 0.0).then_inc(const_ready, 1)
            pool.memset(mask_row[:, :], 0.0).then_inc(const_ready, 1)
            pool.memset(minus_half[:, :], -0.5).then_inc(const_ready, 1)
            pool.wait_ge(const_ready, 3)
            pool.affine_select(out=ident[:, :], in_=ident[:, :], compare_op=ALU.not_equal, fill=1.0, base=0,
                               pattern=[[-1, P]], channel_multiplier=1).then_inc(const_ready, 1)
            tri = mask_row[:, TOKENS - P:TOKENS]
            pool.affine_select(out=tri, in_=tri, compare_op=ALU.is_ge, fill=-3e38, base=0,
                               pattern=[[-1, P]], channel_multiplier=1).then_inc(const_ready, 1)
            for i in range(2):
                split_weights(0, i)
            with pool.Fori(0, BATCH * LAYERS) as it:
                inverse_deviation(it, 0, 0)
                split_weights(it, 2)
                inverse_deviation(it, 0, 1)
                for i in range(3, 6):
                    split_weights(it, i)
                pool.wait_ge(xn_ready, it * 2 * TT + TT)
                pool.wait_ge(bias_loaded, it * 48 + 48)
                for t in range(TT):
                    pool.tensor_tensor(x[:, t, :], x[:, t, :], bias_rows[:, 1, :], ALU.add).then_inc(out_bias_added, 1)
                pool.wait_ge(out_bias_added, it * TT + TT)
                wait_alone(pool, ring_full, full(it, ("v", TT - 1)))
                pool.memset(k_stack[3 * HEAD:3 * HEAD + 2, 0, :, :].bitcast(F32), 1.0).then_inc(ones_ready, 1)
                pool.wait_ge(ones_ready, it + 1)
                for u in range(UNITS):
                    mask_probs(it, u)
                    for i in SPLIT_BESIDE.get(u, ()):
                        split_weights(it, i)
                for c in range(CHUNKS):
                    inverse_deviation(it, 1, c)
                for i in range(11, SLOTS + 2):
                    split_weights(it, i)

        @block.scalar
        def _(act):
            with act.Fori(0, BATCH * LAYERS) as it:
                def xt_to_hi(name):
                    r = name[1]
                    act.wait_ge(ring_full, full(it, name))
                    src = buffer_of(name)[:, :, :].rearrange("p t (k n) -> p k t n", n=P)
                    dst = xt_hi[:, :, 2 * r * P:(2 * r + 2) * P].rearrange("p k (t n) -> p k t n", n=P)
                    act.activation(dst, src, ACT.Copy).then_inc(xt_hi_ready, 1)

                def qk_to_hi(u):
                    g, _ = unit(u)
                    act.wait_ge(ring_full, full(it, ("proj", u)))
                    if u:
                        for h in range(GH):
                            act.wait_ge(kq_stacked[(u - 1) % 2][h], stacked(it, u - 1, len(STACKED)))
                    else:
                        act.wait_ge(bias_loaded, it * 48 + 48)
                    for w in range(2):
                        act.activation(kq_parts[:, 2 - 2 * w, :], buffer_of(("proj", u))[:, w, :], ACT.Identity,
                                       bias=bias_qk[:, w, g:g + 1]).then_inc(qk_hi_ready, 1)

                def exps(u):
                    for j in range(key_tiles(u)):
                        step = J_BASE[u] + j
                        off = max(0, j - CT * unit(u)[1]) * P
                        if step >= 2:
                            act.wait_ge(pv_done, it * KEY_STEPS + step - 1)
                        for h in range(GH):
                            n = GH * step + h
                            act.wait_ge(s2_full, it * S2_STEPS + n + 1)
                            act.activation(prob[:, step % 2, h, off:], bank[n % 2][:, off:], ACT.Exp,
                                           scale=SCALE).then_inc(prob_ready, 1)

                xt_to_hi(("ln1", 0))
                xt_to_hi(("ln1", 1))
                qk_to_hi(0)
                xt_to_hi(("ln1", 2))
                xt_to_hi(("ln1", 3))
                qk_to_hi(1)
                for u in range(UNITS):
                    if u + 2 < UNITS:
                        qk_to_hi(u + 2)
                    exps(u)
                xt_to_hi(("ln2", 0))
                xt_to_hi(("ln2", 1))
                for s in range(STEPS):
                    for t in range(BT):
                        n = s * BT + t
                        act.wait_ge(ring_full, full(it, ("gu", s, t)))
                        if n >= 2:
                            act.wait_ge(ring_drained, drained(it, ("gu", (n - 2) // BT, (n - 2) % BT)))
                        act.activation(silu[:, n % 2, :], buffer_of(("gu", s, t))[:, 0, :], ACT.Silu
                                       ).then_inc(silu_ready, 1)
                    if s == 0:
                        xt_to_hi(("ln2", 2))
                        xt_to_hi(("ln2", 3))

        @block.vector
        def _(dve):
            dve.memset(k_stack[3 * HEAD:3 * HEAD + 2, 1:, :, :].bitcast(F32), 1.0).then_inc(ring_drained, 1)
            dve.memset(ones[:, :], 1.0).then_inc(ring_drained, 1)
            dve.wait_ge(const_ready, CONSTS)

            def iteration(it, b):
                def tile_stats(t):
                    dve.bn_stats(stats[:, t, :], x[:, t, :]).then_inc(stats_done, 1)

                def chunk_variance(ln, c):
                    n = it * 2 * TT + ln * TT + (c + 1) * CT
                    wait_alone(dve, stats_done, 2 * n - CT)
                    for t in range(c * CT, (c + 1) * CT):
                        dve.bn_aggr(mean_var[:, t, :], stats[:, t, :]).then_inc(stats_done, 1)
                    dve.wait_ge(stats_done, 2 * n)
                    t = slice(c * CT, (c + 1) * CT)
                    dve.tensor_scalar(var_eps[:, t], mean_var[:, t, 1], EPS, None, ALU.add).then_inc(var_ready, 1)

                def normalise_pair(ln, r):
                    if r:
                        dve.wait_ge(ring_full, full(it, (f"ln{ln + 1}", r - 1)))
                    dve.wait_ge(rstd_ready, it * 2 * CHUNKS + ln * CHUNKS + 2 * r // CT + 1)
                    for t in (2 * r, 2 * r + 1):
                        dve.tensor_scalar(xn[:, t % 2, :], x[:, t, :], mean_var[:, t, 0:1], rstd[:, t:t + 1],
                                          ALU.subtract, ALU.mult).then_inc(xn_ready, 1)

                def xt_to_lo(ln, r):
                    name = (f"ln{ln + 1}", r)
                    dve.wait_ge(xt_hi_ready, it * TT + ln * (TT // 2) + r + 1)
                    for t in range(2):
                        cols = slice((2 * r + t) * P, (2 * r + t + 1) * P)
                        src = buffer_of(name)[:, t, :].rearrange("p (k n) -> p k n", n=P)
                        ins = dve.tensor_tensor(xt_lo[:, :, cols], src, xt_hi[:, :, cols].bitcast(F32), ALU.subtract)
                    ins.then_inc(ring_drained, 1)

                def take_v(t):
                    dve.wait_ge(ring_full, full(it, ("v", t)))
                    dve.tensor_tensor(v[:, t, :], buffer_of(("v", t))[:, 0, :], bias_rows[:, 0, :], ALU.add
                                      ).then_inc(ring_drained, 1)

                def qk_to_lo(u):
                    g, _ = unit(u)
                    for w in range(2):
                        dve.wait_ge(qk_hi_ready, it * 2 * UNITS + 2 * u + w + 1)
                        part = 2 - 2 * w
                        ins = dve.scalar_tensor_tensor(kq_parts[:, part + 1, :], buffer_of(("proj", u))[:, w, :],
                                                       bias_qk[:, w, g:g + 1], kq_parts[:, part, :].bitcast(F32),
                                                       ALU.add, ALU.subtract)
                    ins.then_inc(ring_drained, 1)

                def maximum(u, s):
                    name = ("s1", u, s)
                    keys = (unit(u)[1] * CT + s % CT + 1) * P
                    src = buffer_of(name)[:, :, :].rearrange("p b n -> p (b n)")
                    wait_alone(dve, ring_full, full(it, name))
                    dve.tensor_tensor_reduce(
                        out=sum_out[:, RING[name] % 2, 0:keys], in0=src[:, 0:keys], in1=mask_row[:, TOKENS - keys:],
                        scale=1.0, scalar=-3.3e38, op0=ALU.add, op1=ALU.max,
                        accum_out=row_max[:, u % 2, s:s + 1]).then_inc(ring_drained, 1)

                def split_max(u):
                    dve.wait_ge(ring_full, full(it, ("mt", u)))
                    src = buffer_of(("mt", u))[0:GH * CT, 0, 0:P]
                    if u:
                        dve.wait_ge(max_stacked[(u - 1) % 2], stacked(it, u - 1, 2))
                    dve.tensor_scalar(nm_hi[:, :], src, -1.0, None, ALU.mult).then_inc(nm_hi_done, 1)
                    dve.wait_ge(nm_hi_done, it * UNITS + u + 1)
                    dve.scalar_tensor_tensor(nm_lo[:, :], src, -1.0, nm_hi[:, :].bitcast(F32), ALU.mult,
                                             ALU.subtract).then_inc(max_split, 1)
                    dve.wait_ge(max_split, it * UNITS + u + 1)
                    dve.tensor_copy(row_max[0:1, u % 2, 0:1], row_max[0:1, u % 2, 0:1]).then_inc(ring_drained, 1)

                def normalise_attn(u):
                    g, c = unit(u)
                    dve.wait_ge(pv_done, it * KEY_STEPS + J_BASE[u] + key_tiles(u))
                    if u:
                        dve.wait_ge(attn_ready, it * UNITS + u)
                    dve.reciprocal(recip[:, :], den_bank[:, :]).then_inc(recip_done, 1)
                    dve.wait_ge(recip_done, it * UNITS + u + 1)
                    dve.tensor_tensor(attn[:, g, c * CHUNK:(c + 1) * CHUNK], out_bank[:, :], recip[:, :], ALU.mult
                                      ).then_inc(attn_ready, 1)

                def split_attn(u):
                    g, c = unit(u)
                    cols = slice(c * CHUNK, (c + 1) * CHUNK)
                    dve.wait_ge(attn_ready, it * UNITS + u + 1)
                    dve.tensor_copy(xt_hi[:, g, cols], attn[:, g, cols]).then_inc(attn_hi_done, 1)
                    dve.wait_ge(attn_hi_done, it * UNITS + u + 1)
                    dve.tensor_tensor(xt_lo[:, g, cols], attn[:, g, cols], xt_hi[:, g, cols].bitcast(F32),
                                      ALU.subtract).then_inc(attn_split, 1)

                def add_rows(row, t, b):
                    dve.wait_ge(rows_full, it * ROWS + row + 1)
                    dve.tensor_tensor(x[:, t, :], x[:, t, :], bank[b][:, :], ALU.add).then_inc(rows_drained, 1)

                def hidden_parts(s, t):
                    n = s * BT + t
                    dve.wait_ge(silu_ready, it * HID_TILES + n + 1)
                    if n >= 2:
                        dve.wait_ge(h_ready, it * HID_TILES + n - 1)
                    dve.tensor_tensor(hidden[:, n % 2, :], silu[:, n % 2, :], buffer_of(("gu", s, t))[:, 1, :], ALU.mult
                                      ).then_inc(ring_drained, 1)
                    dve.wait_ge(ring_drained, drained(it, ("gu", s, t)))
                    hi = h_parts[:, s % 2, 0, t, :]
                    dve.tensor_copy(hi, hidden[:, n % 2, :]).then_inc(h_hi_done, 1)
                    dve.wait_ge(h_hi_done, it * HID_TILES + n + 1)
                    dve.tensor_tensor(h_parts[:, s % 2, 1, t, :], hidden[:, n % 2, :], hi.bitcast(F32), ALU.subtract
                                      ).then_inc(h_ready, 1)

                def down_rows(s):
                    for t in range(CT):
                        add_rows(TT + s * CT + t, s % CHUNKS * CT + t, t)

                def chunk_stats(c):
                    dve.wait_ge(x_loaded[c], b * 16 + 16)
                    for t in range(c * CT, (c + 1) * CT):
                        tile_stats(t)
                    chunk_variance(0, c)

                chunk_stats(0)
                normalise_pair(0, 0)
                normalise_pair(0, 1)
                xt_to_lo(0, 0)
                xt_to_lo(0, 1)
                chunk_stats(1)
                normalise_pair(0, 2)
                dve.wait_ge(bias_loaded, it * 48 + 48)
                for t in range(CT):
                    take_v(t)
                qk_to_lo(0)
                normalise_pair(0, 3)
                xt_to_lo(0, 2)
                xt_to_lo(0, 3)
                qk_to_lo(1)
                take = {"v": take_v, "s1": maximum, "mt": split_max}
                for u in range(-1, UNITS):
                    if u > 0:
                        normalise_attn(u - 1)
                    if 0 <= u < UNITS - 2:
                        qk_to_lo(u + 2)
                    for what, *which in beside(u):
                        take[what](*which)
                for u in range(UNITS - 1):
                    split_attn(u)
                normalise_attn(UNITS - 1)
                split_attn(UNITS - 1)
                dve.wait_ge(out_bias_added, it * TT + TT)
                for c in range(CHUNKS):
                    for t in range(c * CT, (c + 1) * CT):
                        add_rows(t, t, t % 2)
                        dve.wait_ge(rows_drained, it * ROWS + t + 1)
                        tile_stats(t)
                    chunk_variance(1, c)
                normalise_pair(1, 0)
                normalise_pair(1, 1)
                xt_to_lo(1, 0)
                xt_to_lo(1, 1)
                normalise_pair(1, 2)
                for s in range(STEPS):
                    for t in range(BT):
                        hidden_parts(s, t)
                    if s == 0:
                        normalise_pair(1, 3)
                        xt_to_lo(1, 2)
                        xt_to_lo(1, 3)
                    for d in downs_after(s):
                        down_rows(d)

            with dve.Fori(0, BATCH) as b:
                with dve.Fori(0, LAYERS) as layer:
                    iteration(b * LAYERS + layer, b)

        @block.tensor
        def _(pe):
            pe.wait_ge(const_ready, CONSTS)
            pe.wait_ge(ring_drained, RING_CREDIT)

            def iteration(it):
                def three(dst, terms, last_inc=None):
                    n = len(terms)
                    for k, (ah, al, bh, bl) in enumerate(terms):
                        pe.matmul(dst, ah, bh, start=k == 0, stop=False)
                        pe.matmul(dst, ah, bl, start=False, stop=False)
                        ins = pe.matmul(dst, al, bh, start=False, stop=k == n - 1)
                    return ins

                def xt_part(k, cols):
                    return xt_hi[:, k, cols], xt_lo[:, k, cols]

                def transpose_pair(ln, r):
                    name = (f"ln{ln + 1}", r)
                    pe.wait_ge(ring_drained, buffer_free(it, name))
                    pe.wait_ge(xn_ready, it * 2 * TT + ln * TT + 2 * r + 2)
                    for t in range(2):
                        for k in range(KT):
                            ins = pe.transpose(buffer_of(name)[:, t, k * P:(k + 1) * P], xn[:, t, k * P:(k + 1) * P],
                                               ident[:, :])
                    ins.then_inc(ring_full, 1)

                def value_tile(t):
                    pe.wait_ge(ring_drained, buffer_free(it, ("v", t)))
                    pe.wait_ge(ring_drained, drained(it, ("ln1", t // 2)))
                    pe.wait_ge(w_split, it * SLOTS + V_SLOTS[1] + 1)
                    terms = [(*xt_part(k, slice(t * P, (t + 1) * P)),
                              *w_part(V_SLOTS[k // 2], slice(k % 2 * DIM, (k % 2 + 1) * DIM))) for k in range(KT)]
                    three(buffer_of(("v", t))[:, 0, :], terms).then_inc(ring_full, 1)

                def project(u, w):
                    g, c = unit(u)
                    if w == 0:
                        pe.wait_ge(ring_drained, buffer_free(it, ("proj", u)))
                        pe.wait_ge(ring_drained, drained(it, ("ln1", 2 * c + 1)))
                        pe.wait_ge(w_split, it * SLOTS + QK_SLOT0 + g + 1)
                    cols = slice(c * CHUNK, (c + 1) * CHUNK)
                    terms = [(*w_part(QK_SLOT0 + g, slice((2 * k + w) * P, (2 * k + w + 1) * P)), *xt_part(k, cols))
                             for k in range(KT)]
                    ins = three(buffer_of(("proj", u))[:, w, :], terms)
                    if w == 1:
                        ins.then_inc(ring_full, 1)

                def keys_of(u, chunk):
                    return k_buffer(u - unit(u)[1] + chunk)

                def scores(u, s):
                    _, c = unit(u)
                    h, t = divmod(s, CT)
                    if t == 0:
                        pe.wait_ge(kq_stacked[u % 2][h], stacked(it, u, len(STACKED)))
                    pe.wait_ge(ring_drained, buffer_free(it, ("s1", u, s)))
                    q = q_stack[0:3 * HEAD, q_buffer(u), h, t * P:(t + 1) * P]
                    for kc in range(c + 1):
                        n = CHUNK if kc < c else (t + 1) * P
                        ins = pe.matmul(buffer_of(("s1", u, s))[:, kc, 0:n], q,
                                        k_stack[0:3 * HEAD, keys_of(u, kc), h, 0:n], start=True, stop=True)
                    ins.then_inc(ring_full, 1)

                def transpose_max(u):
                    pe.wait_ge(ring_drained, buffer_free(it, ("mt", u)))
                    pe.wait_ge(ring_drained, drained(it, ("s1", u, GH * CT - 1)))
                    pe.transpose(buffer_of(("mt", u))[0:GH * CT, 0, 0:P], row_max[:, u % 2, :], ident[:, :]
                                 ).then_inc(ring_full, 1)

                def scores_t(u, j, h):
                    _, c = unit(u)
                    n = GH * (J_BASE[u] + j) + h
                    off = max(0, j - CT * c) * P
                    if j == 0 and h == 0:
                        pe.wait_ge(max_stacked[u % 2], stacked(it, u, 2))
                        if u == 2:
                            pe.wait_ge(ones_ready, it + 1)
                    if n >= 2:
                        pe.wait_ge(prob_ready, it * S2_STEPS + n - 1)
                    rows = slice(0, 3 * HEAD + 2)
                    pe.matmul(bank[n % 2][:, off:], k_stack[rows, keys_of(u, j // CT), h, j % CT * P:(j % CT + 1) * P],
                              q_stack[rows, q_buffer(u), h, off:], start=True, stop=True).then_inc(s2_full, 1)

                def weigh(u, j, what):
                    g, c = unit(u)
                    step = J_BASE[u] + j
                    d = j - CT * c
                    off = max(0, d) * P
                    if what == "values":
                        pe.wait_ge(prob_ready, it * S2_STEPS + GH * (step + 1))
                        if d >= 0:
                            pe.wait_ge(mask_done, it * UNITS * CT + u * CT + d + 1)
                        if j == 0 and u:
                            pe.wait_ge(attn_ready, it * UNITS + u)
                    for h in range(GH):
                        rows = slice(h * HEAD, (h + 1) * HEAD)
                        dst, a = ((out_bank, v[:, j, g * P + h * HEAD:g * P + (h + 1) * HEAD]) if what == "values"
                                  else (den_bank, ones[:, :]))
                        ins = pe.matmul(dst[rows, off:], a, prob[:, step % 2, h, off:], start=j == 0,
                                        stop=j == key_tiles(u) - 1, tile_position=(0, h * HEAD))
                    if what == "sums":
                        ins.then_inc(pv_done, 1)

                def project_out(t):
                    if t >= 2:
                        pe.wait_ge(rows_drained, it * ROWS + t - 1)
                    if t % CT == 0:
                        pe.wait_ge(attn_split, it * UNITS + (UNITS - 1 if t < CT else UNITS))
                        pe.wait_ge(w_split, it * SLOTS + WO_SLOT0 + 2)
                    cols = slice(t * P, (t + 1) * P)
                    terms = [(*xt_part(g, cols), *w_part(WO_SLOT0 + g // 2, slice(g % 2 * DIM, (g % 2 + 1) * DIM)))
                             for g in range(GROUPS)]
                    three(bank[t % 2][:, :], terms).then_inc(rows_full, 1)

                def gate_up(s):
                    b, c = divmod(s, CHUNKS)
                    cols = slice(c * CHUNK, (c + 1) * CHUNK)
                    if b == 0:
                        pe.wait_ge(ring_drained, drained(it, ("ln2", 2 * c + 1)))
                    if c == 0:
                        pe.wait_ge(w_split, it * SLOTS + FFN_SLOT0 + 3 * b + 2)
                    for t in range(BT):
                        pe.wait_ge(ring_drained, buffer_free(it, ("gu", s, t)))
                        for w in range(2):
                            terms = [(*w_part(FFN_SLOT0 + 3 * b + w, slice(k * BLOCK + t * P, k * BLOCK + (t + 1) * P)),
                                      *xt_part(k, cols)) for k in range(KT)]
                            ins = three(buffer_of(("gu", s, t))[:, w, :], terms)
                        ins.then_inc(ring_full, 1)

                def down(s):
                    b, c = divmod(s, CHUNKS)
                    pe.wait_ge(h_ready, it * HID_TILES + (s + 1) * BT)
                    if c == 0:
                        pe.wait_ge(w_split, it * SLOTS + FFN_SLOT0 + 3 * b + 3)
                    for t in range(CT):
                        row = TT + s * CT + t
                        pe.wait_ge(rows_drained, it * ROWS + (TT if s == 0 else row - CT + 1))
                        tok = slice(t * P, (t + 1) * P)
                        terms = [(h_parts[:, s % 2, 0, i, tok], h_parts[:, s % 2, 1, i, tok],
                                  *w_part(FFN_SLOT0 + 3 * b + 2, slice(i * DIM, (i + 1) * DIM))) for i in range(BT)]
                        three(bank[t][:, :], terms).then_inc(rows_full, 1)

                transpose_pair(0, 0)
                transpose_pair(0, 1)
                for t in range(CT):
                    value_tile(t)
                project(0, 0)
                project(0, 1)
                transpose_pair(0, 2)
                transpose_pair(0, 3)
                project(1, 0)
                project(1, 1)
                run = {"v": value_tile, "s1": scores, "mt": transpose_max}
                for what, *which in beside(-1):
                    run[what](*which)
                for u in range(UNITS):
                    if u + 2 < UNITS:
                        project(u + 2, 0)
                    if u:
                        weigh(u - 1, key_tiles(u - 1) - 1, "values")
                        weigh(u - 1, key_tiles(u - 1) - 1, "sums")
                    if u + 2 < UNITS:
                        project(u + 2, 1)
                    others, done = beside(u), 0
                    points = 4 * key_tiles(u) - TAIL
                    for j in range(key_tiles(u)):
                        for half, what in enumerate(("values", "sums")):
                            for point in range(2):
                                if point == 0:
                                    for h in (2 * half, 2 * half + 1):
                                        scores_t(u, j, h)
                                elif j:
                                    weigh(u, j - 1, what)
                                upto = min(len(others), -(-(4 * j + 2 * half + point + 1) * len(others) // points))
                                for name, *which in others[done:upto]:
                                    run[name](*which)
                                done = upto
                weigh(UNITS - 1, key_tiles(UNITS - 1) - 1, "values")
                weigh(UNITS - 1, key_tiles(UNITS - 1) - 1, "sums")
                for t in range(TT):
                    project_out(t)
                transpose_pair(1, 0)
                transpose_pair(1, 1)
                for s in range(STEPS):
                    gate_up(s)
                    if s == 0:
                        transpose_pair(1, 2)
                        transpose_pair(1, 3)
                    for d in downs_after(s):
                        down(d)

            with pe.Fori(0, BATCH * LAYERS) as it:
                iteration(it)


def lay_out(np, L0_attn_a_x, L0_attn_a_W_qkv, L0_attn_a_b_qkv, L0_attn_a_W_out, L0_attn_a_b_out, L0_attn_b_w_qkv,
            L0_attn_b_b_qkv, L0_attn_b_w_proj, L0_attn_b_b_proj, L0_ffn_w_gate, L0_ffn_w_up, L0_ffn_w_down):
    def row_pairs(w):
        return np.asarray(w).reshape(2, 2, P, DIM).transpose(0, 2, 1, 3).reshape(2, P, SLOT)

    def attn_slots(qkv, proj):
        q, k = (qkv[:, n * DIM:(n + 1) * DIM].reshape(KT, P, GROUPS, 1, P) for n in range(2))
        qk = np.concatenate([q, k], 3).transpose(2, 1, 0, 3, 4).reshape(GROUPS, P, SLOT)
        return np.concatenate([row_pairs(qkv[:, 2 * DIM:]), qk, row_pairs(proj)])

    def column_blocks(w):
        return w.reshape(KT, P, BLOCKS, BLOCK).transpose(2, 1, 0, 3).reshape(BLOCKS, 1, P, SLOT)

    down = L0_ffn_w_down.T.reshape(BLOCKS, 1, BT, P, DIM).transpose(0, 1, 3, 2, 4).reshape(BLOCKS, 1, P, SLOT)
    ffn = np.concatenate([column_blocks(L0_ffn_w_gate.T), column_blocks(L0_ffn_w_up.T), down], 1)
    qkv_biases = (L0_attn_a_b_qkv, L0_attn_b_b_qkv)
    return {
        "x_in": L0_attn_a_x,
        "attn_w": np.stack([attn_slots(L0_attn_a_W_qkv.T, L0_attn_a_W_out.T),
                            attn_slots(L0_attn_b_w_qkv, L0_attn_b_w_proj)]),
        "ffn_w": ffn.reshape(3 * BLOCKS, P, SLOT),
        "qk_bias": np.stack([b[:2 * DIM].reshape(2, GROUPS, P).transpose(2, 0, 1) for b in qkv_biases]),
        "row_bias": np.stack([np.stack([b[2 * DIM:], o])
                              for b, o in zip(qkv_biases, (L0_attn_a_b_out, L0_attn_b_b_proj))]),
    }


def kernel(**inputs):
    import numpy as np
    import concourse.bacc as bacc
    from concourse.bass_utils import run_bass_kernel_spmd

    nc = bacc.Bacc("TRN2", target_bir_lowering=False, num_devices=1)
    laid = {n: np.ascontiguousarray(a) for n, a in lay_out(np, **{n: np.asarray(a) for n, a in inputs.items()}).items()}
    args = [nc.dram_tensor(n, a.shape, mybir.dt.from_np(a.dtype), kind="ExternalInput").ap() for n, a in laid.items()]
    out = nc.dram_tensor("out", (BATCH, TOKENS, DIM), F32, kind="ExternalOutput").ap()
    block_kernel(nc, *args, out)
    r = run_bass_kernel_spmd(nc, [laid], core_ids=[0])
    return r.results[0]["out"]
```

```python
from contextlib import ExitStack

import concourse.bass as bass
from concourse import mybir

F32 = mybir.dt.float32
F32R = mybir.dt.float32r
BF16 = mybir.dt.bfloat16
ALU = mybir.AluOpType
ACT = mybir.ActivationFunctionType

P = 128
BATCH, TOKENS, DIM, HIDDEN, HEADS = 2, 1024, 512, 2048, 16
LAYERS = 2
HEAD = DIM // HEADS
SCALE = float(HEAD) ** -0.5
EPS = 1e-5
KT = DIM // P
TT = TOKENS // P
CHUNK = 512
CT = CHUNK // P
CHUNKS = TOKENS // CHUNK
GH = P // HEAD
GROUPS = HEADS // GH
UNITS = GROUPS * CHUNKS
BLOCK = 256
BT = BLOCK // P
BLOCKS = HIDDEN // BLOCK
STEPS = BLOCKS * CHUNKS

SLOT = 1024
V_SLOTS, QK_SLOT0, WO_SLOT0, FFN_SLOT0 = (0, 1), 2, 2 + GROUPS, 4 + GROUPS
SLOTS = FFN_SLOT0 + 3 * BLOCKS
SPLIT_BEFORE = {1: QK_SLOT0 + 2, 2: QK_SLOT0 + 3, 3: WO_SLOT0, 4: WO_SLOT0 + 1, 5: FFN_SLOT0, 7: FFN_SLOT0 + 1}
LOAD_BESIDE = {1: WO_SLOT0, 2: WO_SLOT0 + 1, 3: FFN_SLOT0, 4: FFN_SLOT0 + 1, 6: FFN_SLOT0 + 2}
PLACES = 5
LENT_PLACES = (0, 1)
ATTN_PLACES = (2, 4, 3, 3, 2, 4, 3, 2)
FFN_PLACES = (4, 1, 0, 3, 2)
AHEAD = QK_SLOT0 + 1


def place(i):
    return ATTN_PLACES[i] if i < FFN_SLOT0 else FFN_PLACES[(i - FFN_SLOT0) % PLACES]


def slot_before(i):
    return max((j for j in range(i) if place(j) == place(i)), default=None)


def unit(u):
    return u // CHUNKS, u % CHUNKS


def key_tiles(u):
    return CT * (unit(u)[1] + 1)


def downs_after(s):
    return {0: (0,), 1: (), STEPS - 2: (s - 1, s), STEPS - 1: (s,)}.get(s, (s - 1,))


EARLY = {1: 2, 3: 12, 5: 12, 7: 14}


def beside(u):
    if u == UNITS - 1:
        return [("op", t) for t in range(CT)] + [("ln2", 0), ("ln2", 1)]
    tiles = [("s1", u + 1, s) for s in range(GH * CT)][EARLY.get(u + 1, 0):]
    ahead = [("s1", u + 2, s) for s in range(EARLY.get(u + 2, 0))]
    return tiles + ahead[:1] + [("mt", u + 1)] + ahead[1:]


def points(u):
    if u == UNITS - 1:
        return [9, 11, 13, 15, 23, 27]
    n = len(beside(u)) - sum(BETWEEN.get(u, ()))
    first = FIRST[unit(u)[1]]
    return [first + i * (4 * (key_tiles(u) - 1) - TAIL - first) // n for i in range(n)]


SIDE_UNITS = (2, *range(3, UNITS, 2))
SIDE_ORDER = [("v", t) for t in range(CT, TT)] + [(w, u) for u in SIDE_UNITS for w in "qk"]
SIDE = {name: n for n, name in enumerate(SIDE_ORDER)}
SIDE_USES = len(SIDE)


def ring_order():
    yield from (("ln1", 0), ("ln1", 1), *(("v", t) for t in range(CT)))
    yield from (("q", 0), ("ln1", 2), ("k", 0), ("ln1", 3), ("q", 1), ("k", 1))
    for u in range(-1, UNITS):
        if 0 <= u < UNITS - 2 and u + 2 not in SIDE_UNITS:
            yield from (("q", u + 2), ("k", u + 2))
        yield from beside(u)
    yield ("gu", 0, 0)
    yield from (("op", t) for t in range(CT, TT))
    yield from (("gu", 0, 1), ("ln2", 2), ("ln2", 3))
    yield from (("gu", s, t) for s in range(1, STEPS) for t in range(BT))


TAKE_AFTER = (8, 17)
RECIPS = 8
AFTER_STORE = 2
BETWEEN = {0: (2, 1, 2, 1), 1: (2, 1, 2, 1), 3: (2, 1, 2, 1), 5: (2, 1, 2, 1)}
LO_BEFORE = {0: (2, 5), 1: (2, 5), 3: (2, 5), 5: (2, 5)}
RECIPS_FROM = 6
RECIPS_BETWEEN = 6
FIRST = (0, 1)
TAIL = 1
RING = {name: n for n, name in enumerate(ring_order())}
RING_USES = len(RING)
assert RING_USES % 2 == 0 and SLOTS % 2 == 0
J_BASE = [sum(key_tiles(v) for v in range(u)) for u in range(UNITS)]
KEY_STEPS = sum(key_tiles(u) for u in range(UNITS))
S2_STEPS = GH * KEY_STEPS
ROWS = STEPS * CT
HID_TILES = STEPS * BT
K_BUFS, Q_BUFS = 4, 3
PLACE_AT = (0, *range(K_BUFS + Q_BUFS - 1, K_BUFS + Q_BUFS + PLACES - len(LENT_PLACES)))
STACKED = ((0, 2), (0, 3), (1, 2))


def block_kernel(nc, x_in, attn_w, ffn_w, qk_bias, row_bias, out):
    with ExitStack() as ctx:
        def sb(name, shape, dt=F32):
            return ctx.enter_context(nc.sbuf_tensor(name, shape, dt))

        def sem(name):
            return ctx.enter_context(nc.semaphore(name))

        x = sb("x", [P, TT, DIM])
        xt_hi = sb("xt_hi", [P, KT, TOKENS], F32R)
        xt_lo = sb("xt_lo", [P, KT, TOKENS], F32R)
        v = sb("v", [P, TT, DIM])
        attn = sb("attn", [P, GROUPS, TOKENS])
        area = sb("area", [P, K_BUFS + Q_BUFS + PLACES - len(LENT_PLACES), 2 * SLOT], F32R)
        kq_stack = area[:, 0:K_BUFS + Q_BUFS, :].rearrange("p b (h n) -> p b h n", h=GH)
        k_stack = kq_stack[:, 0:K_BUFS, :, :]
        q_stack = kq_stack[:, K_BUFS:, :, :]
        h_parts = q_stack[:, 0:2, :, :].rearrange("p b (s t) n -> p b s t n", s=2)
        prob = sb("prob", [P, 2, GH, CHUNK])
        silu = prob[:, 0, 0:2, :]
        hidden = prob[:, 1, 0:2, :]
        kq_parts = sb("kq_parts", [P, 4, CHUNK], F32R)
        mask_row = sb("mask_row", [P, TOKENS], BF16)
        xn = sb("xn", [P, 2, DIM])
        sum_out = xn[:, :, :].bitcast(BF16)
        w_stage = sb("w_stage", [P, 2, SLOT])
        table_out = sb("table_out", [1, 1])
        recip = sb("recip", [P, CHUNK])
        bias_rows = sb("bias_rows", [P, 2, DIM])
        bias_qk = sb("bias_qk", [P, 2, GROUPS])
        ident = sb("ident", [P, P])
        ones = sb("ones", [P, HEAD])
        row_max = sb("row_max", [P, 2, GH * CT])
        nm_hi = sb("nm_hi", [GH * CT, P], F32R)
        nm_lo = sb("nm_lo", [GH * CT, P], F32R)
        stats = sb("stats", [P, TT, 6])
        mean_var = sb("mean_var", [P, TT, 2])
        var_eps = sb("var_eps", [P, TT])
        rstd = sb("rstd", [P, TT])
        minus_half = sb("minus_half", [P, CT])

        ring = [ctx.enter_context(nc.psum_tensor(f"ring{i}", [P, 2, CHUNK], F32)) for i in range(2)]
        bank = [ctx.enter_context(nc.psum_tensor(f"bank{i}", [P, CHUNK], F32)) for i in range(4)]
        out_bank, den_bank = bank[2], bank[3]

        x_loaded = [sem(f"x_loaded{c}") for c in range(CHUNKS)]
        x_stored = [sem(f"x_stored{t}") for t in range(TT)]
        bias_loaded = sem("bias_loaded")
        w_loaded = [sem("w_loaded0"), sem("w_loaded1")]
        kq_stacked = [[sem(f"kq_stacked{n}_{h}") for h in range(GH)] for n in range(2)]
        max_stacked = [sem("max_stacked0"), sem("max_stacked1")]
        const_ready, w_split, w_hi_done = sem("const_ready"), sem("w_split"), sem("w_hi_done")
        rstd_ready, out_bias_added, mask_done = sem("rstd_ready"), sem("out_bias_added"), sem("mask_done")
        ones_ready, attn_hi_done, attn_split = sem("ones_ready"), sem("attn_hi_done"), sem("attn_split")
        ring_full, s2_full, pv_done, rows_full = sem("ring_full"), sem("s2_full"), sem("pv_done"), sem("rows_full")
        side_full = sem("side_full")
        xt_hi_ready, qk_hi_ready, prob_ready, silu_ready = (
            sem("xt_hi_ready"), sem("qk_hi_ready"), sem("prob_ready"), sem("silu_ready"))
        evacuated = sem("evacuated")
        ring_drained, stats_done, var_ready, xn_ready = (
            sem("ring_drained"), sem("stats_done"), sem("var_ready"), sem("xn_ready"))
        max_ready, nm_hi_done, max_split, recip_done = (
            sem("max_ready"), sem("nm_hi_done"), sem("max_split"), sem("recip_done"))
        side_taken = sem("side_taken")
        attn_ready, last_hi_done, last_split = sem("attn_ready"), sem("last_hi_done"), sem("last_split")
        h_hi_done, h_ready, rows_drained = sem("h_hi_done"), sem("h_ready"), sem("rows_drained")

        def projected(u, w):
            if u == 2:
                return bank[2 + w][:, :]
            if u in SIDE_UNITS:
                return ring[(RING["mt", u - 2] + w) % 2][:, 1, :]
            return buffer_of(("qk"[w], u))[:, 0, :]

        def side_done(it, name):
            return it * SIDE_USES + SIDE[name] + 1

        def wait_projected(wait, it, u, w):
            name = ("qk"[w], u)
            if name in SIDE:
                wait(side_full, side_done(it, name))
            else:
                wait(ring_full, full(it, name))

        RING_CREDIT = 2

        def parts_of(u):
            if u == 1:
                return attn[:, 2:4, :].rearrange("p g (s n) -> p (g s) n", n=CHUNK).bitcast(F32R)
            return kq_parts

        def k_buffer(u):
            return (u - 2) % K_BUFS

        def q_buffer(u):
            return u % Q_BUFS

        def xn_tile(t):
            return xn[:, t % 2, :] if t % 4 < 2 else attn[:, t % 2, 0:DIM]

        def buffer_of(name):
            return ring[RING[name] % 2]

        def full(it, name):
            return it * RING_USES + RING[name] + 1

        def drained(it, name):
            return it * RING_USES + RING[name] + 1 + RING_CREDIT

        def buffer_free(it, name):
            return it * RING_USES + RING[name] - 1 + RING_CREDIT

        def stacked(it, u, each):
            return 16 * each * (it * (UNITS // 2) + u // 2 + 1)

        def w_part(slot, cols):
            at = PLACE_AT[place(slot)]
            return area[:, at, cols], area[:, at, cols.start + SLOT:cols.stop + SLOT]

        CONSTS = 5

        def wait_alone(eng, semaphore, value):
            if not isinstance(value, int):
                value = eng.snap(eng.to_reg(value))
            eng.wait_ge(const_ready, CONSTS)
            eng.wait_ge(semaphore, value)

        block = ctx.enter_context(nc.Block())

        @block.sync
        def _(sp):
            def load_weights(i, it, attn_src):
                if i >= 2 or it is not None:
                    wait_alone(sp, w_split, (0 if it is None else it * SLOTS) + i - 1)
                j = i % SLOTS
                src = attn_src[j] if j < FFN_SLOT0 else ffn_w[j - FFN_SLOT0]
                sp.dma_start(w_stage[:, j % 2, :], src).then_inc(w_loaded[j % 2], 16)

            def load_biases(layer):
                sp.dma_start(bias_qk[:, :, :], qk_bias[layer]).then_inc(bias_loaded, 16)
                for r in range(2):
                    sp.dma_start(bias_rows[:, r, :], row_bias[layer, r:r + 1, :].to_broadcast([P, DIM])
                                 ).then_inc(bias_loaded, 16)

            def stack_qk(it, u):
                if u in SIDE_UNITS:
                    wait_alone(sp, side_taken, side_done(it, ("k", u)))
                else:
                    wait_alone(sp, ring_drained, drained(it, ("k", u)))
                kb, qb = k_buffer(u), K_BUFS + q_buffer(u)
                for h in range(GH):
                    rows = slice(h * HEAD, (h + 1) * HEAD)
                    for n, (k, q) in enumerate(STACKED):
                        src = parts_of(u)[rows, k:q + 1:q - k, :].bitcast(F32)
                        dst = kq_stack[n * HEAD:(n + 1) * HEAD, kb:qb + 1:qb - kb, h, :].bitcast(F32)
                        sp.dma_start(dst, src).then_inc(kq_stacked[u % 2][h], 16)

            def stack_max(it, u):
                wait_alone(sp, max_split, it * UNITS + u + 1)
                for r, part in ((3 * HEAD, nm_hi), (3 * HEAD + 1, nm_lo)):
                    row = q_stack[r:r + 1, q_buffer(u), :, :].rearrange("p h (t n) -> p (h t) n", n=P)
                    sp.dma_start(row.bitcast(F32), part[:, :].bitcast(F32)).then_inc(max_stacked[u % 2], 16)

            def load_x(batch, c):
                for t in range(c * CT, (c + 1) * CT):
                    sp.dma_start(x[:, t, :], x_in[batch, t * P:(t + 1) * P, :]).then_inc(x_loaded[c], 16)

            load_x(0, 0)
            for i in range(2):
                load_weights(i, None, attn_w[0])
            load_x(0, 1)
            load_biases(0)
            for i in range(2, AHEAD):
                load_weights(i, None, attn_w[0])
            with sp.Fori(0, BATCH) as b:
                with sp.Fori(0, LAYERS) as layer:
                    it = b * LAYERS + layer
                    own, other = attn_w[layer], attn_w[1 - layer]
                    for i in range(AHEAD, AHEAD + 2):
                        load_weights(i, it, own)
                    stack_qk(it, 0)
                    stack_qk(it, 1)
                    load_weights(AHEAD + 2, it, own)
                    stack_max(it, 0)
                    for u in range(UNITS - 1):
                        if u + 2 < UNITS:
                            stack_qk(it, u + 2)
                        stack_max(it, u + 1)
                        if u in LOAD_BESIDE:
                            load_weights(LOAD_BESIDE[u], it, own)
                    load_weights(11, it, own)
                    wait_alone(sp, out_bias_added, it * TT + TT)
                    load_biases(1 - layer)
                    for i in range(12, SLOTS + AHEAD):
                        load_weights(i, it, own if i < SLOTS else other)
                for c in range(CHUNKS):
                    for n in range(CT + AFTER_STORE):
                        if n < CT:
                            t = c * CT + n
                            wait_alone(sp, rows_drained, (b * LAYERS + LAYERS) * ROWS - TT + t + 1)
                            sp.dma_start(out[b, t * P:(t + 1) * P, :], x[:, t, :]).then_inc(x_stored[t], 16)
                        if n >= AFTER_STORE:
                            t = c * CT + n - AFTER_STORE
                            wait_alone(sp, x_stored[t], b * 16 + 16)
                            sp.dma_start(x[:, t, :], x_in[BATCH - 1, t * P:(t + 1) * P, :]).then_inc(x_loaded[c], 16)
            for s in x_loaded:
                sp.wait_ge(s, 16 * CT * (BATCH + 1))
            sp.wait_ge(w_loaded[0], 16 * (BATCH * LAYERS * SLOTS // 2 + AHEAD - AHEAD // 2))
            for s in w_loaded[1:]:
                sp.wait_ge(s, 16 * (BATCH * LAYERS * SLOTS // 2 + AHEAD // 2))
            sp.wait_ge(bias_loaded, 48 * (BATCH * LAYERS + 1))

        @block.gpsimd
        def _(pool):
            def split_weights(it, i):
                j = i % SLOTS
                n = it * SLOTS + i
                wait_alone(pool, w_loaded[j % 2], (it * (SLOTS // 2) + i // 2 + 1) * 16)
                before = slot_before(j)
                if i >= SLOTS:
                    before = max(q for q in range(SLOTS) if place(q) == place(j))
                if before is not None:
                    after = last_product(before)
                    if after[0] == "rows":
                        wait_alone(pool, rows_full, it * ROWS + after[1] + 1)
                    elif after in SIDE:
                        wait_alone(pool, side_full, side_done(it, after))
                    else:
                        wait_alone(pool, ring_full, full(it, after))
                elif place(j) in LENT_PLACES:
                    lent_steps = KEY_STEPS if place(j) == 0 else J_BASE[6]
                    wait_alone(pool, s2_full, it * S2_STEPS + GH * lent_steps)
                hi, lo, src = *w_part(j, slice(0, SLOT)), w_stage[:, j % 2, :]
                pool.tensor_scalar(hi, src, 1.0, 0.0, ALU.mult, ALU.add).then_inc(w_hi_done, 1)
                pool.wait_ge(w_hi_done, n + 1)
                pool.tensor_tensor(lo, src, hi.bitcast(F32), ALU.subtract).then_inc(w_split, 1)

            def last_product(i):
                if i in V_SLOTS:
                    return ("v", TT - 1)
                if i < WO_SLOT0:
                    return ("k", (i - QK_SLOT0) * CHUNKS + CHUNKS - 1)
                if i < FFN_SLOT0:
                    return ("op", TT - 1)
                b, part = divmod(i - FFN_SLOT0, 3)
                x_last = b * CHUNKS + CHUNKS - 1
                return ("rows", x_last * CT + CT - 1) if part == 2 else ("gu", x_last, BT - 1)

            def inverse_deviation(it, ln, c):
                n = it * 2 * CHUNKS + ln * CHUNKS + c + 1
                pool.wait_ge(var_ready, n)
                t = slice(c * CT, (c + 1) * CT)
                pool.tensor_tensor(rstd[:, t], var_eps[:, t], minus_half[:, :], ALU.pow).then_inc(rstd_ready, 1)

            def mask_probs(it, u, d):
                step = J_BASE[u] + key_tiles(u) - CT + d
                wait_alone(pool, prob_ready, it * S2_STEPS + GH * (step + 1))
                tile = prob[:, step % 2, :, d * P:(d + 1) * P]
                pool.affine_select(out=tile, in_=tile, compare_op=ALU.is_ge, fill=0.0, base=0,
                                   pattern=[[0, GH], [1, P]], channel_multiplier=-1).then_inc(mask_done, 1)

            def split_attn(it, u):
                g, c = unit(u)
                cols = slice(c * CHUNK, (c + 1) * CHUNK)
                wait_alone(pool, side_full, side_done(it, ("k", UNITS - 1)))
                wait_alone(pool, attn_ready, it * UNITS + u + 1)
                pool.tensor_scalar(xt_hi[:, g, cols], attn[:, g, cols], 1.0, 0.0, ALU.mult, ALU.add
                                   ).then_inc(attn_hi_done, 1)
                pool.wait_ge(attn_hi_done, it * (UNITS - 1) + u + 1)
                pool.tensor_tensor(xt_lo[:, g, cols], attn[:, g, cols], xt_hi[:, g, cols].bitcast(F32), ALU.subtract
                                   ).then_inc(attn_split, 1)

            pool.memset(ident[:, :], 0.0).then_inc(const_ready, 1)
            pool.memset(mask_row[:, :], 0.0).then_inc(const_ready, 1)
            pool.memset(minus_half[:, :], -0.5).then_inc(const_ready, 1)
            pool.wait_ge(const_ready, 3)
            pool.affine_select(out=ident[:, :], in_=ident[:, :], compare_op=ALU.not_equal, fill=1.0, base=0,
                               pattern=[[-1, P]], channel_multiplier=1).then_inc(const_ready, 1)
            tri = mask_row[:, TOKENS - P:TOKENS]
            pool.affine_select(out=tri, in_=tri, compare_op=ALU.is_ge, fill=-3e38, base=0,
                               pattern=[[-1, P]], channel_multiplier=1).then_inc(const_ready, 1)
            split_weights(0, 0)
            inverse_deviation(0, 0, 0)
            for i in range(1, AHEAD):
                split_weights(0, i)
            with pool.Fori(0, BATCH * LAYERS) as it:
                inverse_deviation(it, 0, 1)
                split_weights(it, AHEAD)
                pool.wait_ge(xn_ready, it * 2 * TT + TT)
                pool.wait_ge(bias_loaded, it * 48 + 48)
                for t in range(TT):
                    pool.tensor_tensor(x[:, t, :], x[:, t, :], bias_rows[:, 1, :], ALU.add).then_inc(out_bias_added, 1)
                wait_alone(pool, out_bias_added, it * TT + TT)
                pool.memset(k_stack[3 * HEAD:3 * HEAD + 2, 0, :, :].bitcast(F32), 1.0).then_inc(ones_ready, 1)
                pool.wait_ge(ones_ready, it + 1)
                for u in range(UNITS):
                    if u in SPLIT_BEFORE:
                        split_weights(it, SPLIT_BEFORE[u])
                    for w in {5: range(5), 7: range(5, 7)}.get(u, ()):
                        split_attn(it, w)
                    for d in range(CT):
                        mask_probs(it, u, d)
                        if u == UNITS - 1 and d == 1:
                            inverse_deviation(it, 1, 0)
                split_weights(it, FFN_SLOT0 + 2)
                inverse_deviation(it, 1, 1)
                for i in range(FFN_SLOT0 + 3, SLOTS + 2):
                    split_weights(it, i)
                inverse_deviation(it + 1, 0, 0)
                for i in range(SLOTS + 2, SLOTS + AHEAD):
                    split_weights(it, i)

        @block.scalar
        def _(act):
            def xt_to_hi(it, name):
                r = name[1]
                act.wait_ge(ring_full, full(it, name))
                src = buffer_of(name)[:, :, :].rearrange("p t (k n) -> p k t n", n=P)
                dst = xt_hi[:, :, 2 * r * P:(2 * r + 2) * P].rearrange("p k (t n) -> p k t n", n=P)
                act.activation(dst, src, ACT.Copy).then_inc(xt_hi_ready, 1)

            def iteration(it):
                def qk_to_hi(u, w):
                    g, _ = unit(u)
                    wait_projected(act.wait_ge, it, u, w)
                    if u >= 2 and w == 0:
                        before = u - 1 if u > 2 else 0
                        for h in range(GH):
                            act.wait_ge(kq_stacked[before % 2][h], stacked(it, before, len(STACKED)))
                    elif u == 0 and w == 0:
                        act.wait_ge(bias_loaded, it * 48 + 48)
                    act.activation(parts_of(u)[:, 2 - 2 * w, :], projected(u, w), ACT.Identity,
                                   bias=bias_qk[:, w, g:g + 1]).then_inc(qk_hi_ready, 1)

                def exps(u, j, heads):
                    step = J_BASE[u] + j
                    off = max(0, j - CT * unit(u)[1]) * P
                    if step >= 2:
                        act.wait_ge(pv_done, it * KEY_STEPS + step - 1)
                    for h in heads:
                        n = GH * step + h
                        act.wait_ge(s2_full, it * S2_STEPS + n + 1)
                        act.activation(prob[:, step % 2, h, off:], bank[n % 2][:, off:], ACT.Exp,
                                       scale=SCALE).then_inc(prob_ready, 1)

                def evacuate(u):
                    g, c = unit(u)
                    act.wait_ge(pv_done, it * KEY_STEPS + J_BASE[u] + key_tiles(u))
                    if u:
                        act.wait_ge(attn_ready, it * UNITS + u)
                    act.activation(recip[:, :], den_bank[:, :], ACT.Copy)
                    act.activation(attn[:, g, c * CHUNK:(c + 1) * CHUNK], out_bank[:, :], ACT.Copy
                                   ).then_inc(evacuated, 1)

                def silus(s, t):
                    n = s * BT + t
                    act.wait_ge(ring_full, full(it, ("gu", s, t)))
                    if n >= 2:
                        act.wait_ge(ring_drained, drained(it, ("gu", (n - 2) // BT, (n - 2) % BT)))
                    act.activation(silu[:, n % 2, :], buffer_of(("gu", s, t))[:, 0, :], ACT.Silu
                                   ).then_inc(silu_ready, 1)

                qk_to_hi(0, 0)
                xt_to_hi(it, ("ln1", 2))
                qk_to_hi(0, 1)
                xt_to_hi(it, ("ln1", 3))
                qk_to_hi(1, 0)
                qk_to_hi(1, 1)
                for u in range(UNITS):
                    if u + 2 < UNITS:
                        if u:
                            evacuate(u - 1)
                        qk_to_hi(u + 2, 0)
                        exps(u, 0, range(GH))
                        qk_to_hi(u + 2, 1)
                    else:
                        if u == UNITS - 1:
                            evacuate(u - 1)
                        exps(u, 0, range(0, 2))
                        if u < UNITS - 1:
                            evacuate(u - 1)
                        exps(u, 0, range(2, GH))
                    for j in range(1, key_tiles(u)):
                        exps(u, j, range(GH))
                        if u == UNITS - 1 and j >= key_tiles(u) - 2:
                            xt_to_hi(it, ("ln2", j - key_tiles(u) + 2))
                load_table(ACT.Silu)
                evacuate(UNITS - 1)
                silus(0, 0)
                silus(0, 1)
                xt_to_hi(it, ("ln2", 2))
                xt_to_hi(it, ("ln2", 3))
                for s in range(1, STEPS):
                    for t in range(BT):
                        silus(s, t)
                load_table(ACT.Exp)
                xt_to_hi(it + 1, ("ln1", 0))
                xt_to_hi(it + 1, ("ln1", 1))

            def load_table(func):
                act.activation(table_out[:, :], ident[0:1, 0:1], func)

            act.wait_ge(const_ready, CONSTS)
            load_table(ACT.Exp)
            xt_to_hi(0, ("ln1", 0))
            xt_to_hi(0, ("ln1", 1))
            with act.Fori(0, BATCH * LAYERS) as it:
                iteration(it)

        @block.vector
        def _(dve):
            dve.memset(k_stack[3 * HEAD:3 * HEAD + 2, 1:, :, :].bitcast(F32), 1.0).then_inc(ring_drained, 1)
            dve.memset(ones[:, :], 1.0).then_inc(ring_drained, 1)
            dve.wait_ge(const_ready, CONSTS)

            def tile_stats(t):
                dve.bn_stats(stats[:, t, :], x[:, t, :]).then_inc(stats_done, 1)

            def chunk_variance(it, ln, c):
                n = it * 2 * TT + ln * TT + (c + 1) * CT
                wait_alone(dve, stats_done, 2 * n - CT)
                for t in range(c * CT, (c + 1) * CT):
                    dve.bn_aggr(mean_var[:, t, :], stats[:, t, :]).then_inc(stats_done, 1)
                dve.wait_ge(stats_done, 2 * n)
                t = slice(c * CT, (c + 1) * CT)
                dve.tensor_scalar(var_eps[:, t], mean_var[:, t, 1], EPS, None, ALU.add).then_inc(var_ready, 1)

            def chunk_stats(it, c, loads):
                dve.wait_ge(x_loaded[c], loads * (16 * CT))
                for t in range(c * CT, (c + 1) * CT):
                    tile_stats(t)
                chunk_variance(it, 0, c)

            def normalise_pair(it, ln, r):
                if r >= 2:
                    dve.wait_ge(ring_full, full(it, (f"ln{ln + 1}", r - 2)))
                dve.wait_ge(rstd_ready, it * 2 * CHUNKS + ln * CHUNKS + 2 * r // CT + 1)
                for t in (2 * r, 2 * r + 1):
                    dve.tensor_scalar(xn_tile(t), x[:, t, :], mean_var[:, t, 0:1], rstd[:, t:t + 1],
                                      ALU.subtract, ALU.mult).then_inc(xn_ready, 1)

            def xt_to_lo(it, ln, r):
                name = (f"ln{ln + 1}", r)
                dve.wait_ge(xt_hi_ready, it * TT + ln * (TT // 2) + r + 1)
                for t in range(2):
                    cols = slice((2 * r + t) * P, (2 * r + t + 1) * P)
                    src = buffer_of(name)[:, t, :].rearrange("p (k n) -> p k n", n=P)
                    ins = dve.tensor_tensor(xt_lo[:, :, cols], src, xt_hi[:, :, cols].bitcast(F32), ALU.subtract)
                ins.then_inc(ring_drained, 1)

            def iteration(it, b, layer):
                def take_v(t):
                    if t < CT:
                        dve.wait_ge(ring_full, full(it, ("v", t)))
                        src, taken = buffer_of(("v", t))[:, 0, :], ring_drained
                    else:
                        dve.wait_ge(side_full, side_done(it, ("v", t)))
                        src, taken = bank[t - CT][:, :], side_taken
                    dve.tensor_tensor(v[:, t, :], src, bias_rows[:, 0, :], ALU.add).then_inc(taken, 1)

                def qk_to_lo(u, w):
                    g, _ = unit(u)
                    part = 2 - 2 * w
                    dve.wait_ge(qk_hi_ready, it * 2 * UNITS + 2 * u + w + 1)
                    dve.scalar_tensor_tensor(parts_of(u)[:, part + 1, :], projected(u, w), bias_qk[:, w, g:g + 1],
                                             parts_of(u)[:, part, :].bitcast(F32), ALU.add, ALU.subtract
                                             ).then_inc(side_taken if u in SIDE_UNITS else ring_drained, 1)

                def maximum(u, s):
                    name = ("s1", u, s)
                    keys = (unit(u)[1] * CT + s % CT + 1) * P
                    src = buffer_of(name)[:, :, :].rearrange("p b n -> p (b n)")
                    wait_alone(dve, ring_full, full(it, name))
                    dve.tensor_tensor_reduce(
                        out=sum_out[:, RING[name] % 2, 0:keys], in0=src[:, 0:keys], in1=mask_row[:, TOKENS - keys:],
                        scale=1.0, scalar=-3.3e38, op0=ALU.add, op1=ALU.max,
                        accum_out=row_max[:, u % 2, s:s + 1]).then_inc(ring_drained, 1)

                def split_max(u):
                    dve.wait_ge(ring_full, full(it, ("mt", u)))
                    src = buffer_of(("mt", u))[0:GH * CT, 0, 0:P]
                    if u:
                        dve.wait_ge(max_stacked[(u - 1) % 2], stacked(it, u - 1, 2))
                    dve.tensor_scalar(nm_hi[:, :], src, -1.0, None, ALU.mult).then_inc(nm_hi_done, 1)
                    dve.wait_ge(nm_hi_done, it * UNITS + u + 1)
                    dve.scalar_tensor_tensor(nm_lo[:, :], src, -1.0, nm_hi[:, :].bitcast(F32), ALU.mult,
                                             ALU.subtract).then_inc(max_split, 1)
                    dve.wait_ge(max_split, it * UNITS + u + 1)
                    dve.tensor_copy(row_max[0:1, u % 2, 0:1], row_max[0:1, u % 2, 0:1]).then_inc(ring_drained, 1)

                def recip_part(u, n):
                    if n == 0:
                        dve.wait_ge(evacuated, it * UNITS + u + 1)
                    cols = slice(n * CHUNK // RECIPS, (n + 1) * CHUNK // RECIPS)
                    dve.reciprocal(recip[:, cols], recip[:, cols]).then_inc(recip_done, 1)

                def normalise_attn(u):
                    g, c = unit(u)
                    cols = slice(c * CHUNK, (c + 1) * CHUNK)
                    dve.wait_ge(recip_done, (it * UNITS + u + 1) * RECIPS)
                    dve.tensor_tensor(attn[:, g, cols], attn[:, g, cols], recip[:, :], ALU.mult).then_inc(attn_ready, 1)

                def split_last():
                    g, c = unit(UNITS - 1)
                    cols = slice(c * CHUNK, (c + 1) * CHUNK)
                    dve.wait_ge(attn_ready, it * UNITS + UNITS)
                    dve.tensor_copy(xt_hi[:, g, cols], attn[:, g, cols]).then_inc(last_hi_done, 1)
                    dve.wait_ge(last_hi_done, it + 1)
                    dve.tensor_tensor(xt_lo[:, g, cols], attn[:, g, cols], xt_hi[:, g, cols].bitcast(F32),
                                      ALU.subtract).then_inc(last_split, 1)

                def add_projected(t):
                    name = ("op", t)
                    dve.wait_ge(ring_full, full(it, name))
                    if t == 0:
                        dve.wait_ge(out_bias_added, it * TT + TT)
                    dve.tensor_tensor(x[:, t, :], x[:, t, :], buffer_of(name)[:, 0, :], ALU.add).then_inc(ring_drained, 1)
                    dve.wait_ge(ring_drained, drained(it, name))
                    tile_stats(t)

                def add_rows(row, t, b):
                    dve.wait_ge(rows_full, it * ROWS + row + 1)
                    dve.tensor_tensor(x[:, t, :], x[:, t, :], bank[b][:, :], ALU.add).then_inc(rows_drained, 1)

                def hidden_parts(s, t):
                    n = s * BT + t
                    dve.wait_ge(silu_ready, it * HID_TILES + n + 1)
                    if n >= 2:
                        dve.wait_ge(h_ready, it * HID_TILES + n - 1)
                    dve.tensor_tensor(hidden[:, n % 2, :], silu[:, n % 2, :], buffer_of(("gu", s, t))[:, 1, :], ALU.mult
                                      ).then_inc(ring_drained, 1)
                    dve.wait_ge(ring_drained, drained(it, ("gu", s, t)))
                    hi = h_parts[:, s % 2, 0, t, :]
                    dve.tensor_copy(hi, hidden[:, n % 2, :]).then_inc(h_hi_done, 1)
                    dve.wait_ge(h_hi_done, it * HID_TILES + n + 1)
                    dve.tensor_tensor(h_parts[:, s % 2, 1, t, :], hidden[:, n % 2, :], hi.bitcast(F32), ALU.subtract
                                      ).then_inc(h_ready, 1)

                def down_rows(s):
                    for t in range(CT):
                        add_rows(s * CT + t, s % CHUNKS * CT + t, t)

                chunk_stats(it, 1, b + 1)
                dve.wait_ge(bias_loaded, it * 48 + 48)
                take_v(0)
                normalise_pair(it, 0, 2)
                normalise_pair(it, 0, 3)
                for t in range(1, CT):
                    take_v(t)
                qk_to_lo(0, 0)
                xt_to_lo(it, 0, 2)
                qk_to_lo(0, 1)
                xt_to_lo(it, 0, 3)
                take_v(CT)
                qk_to_lo(1, 0)
                qk_to_lo(1, 1)
                take_v(CT + 1)
                take = {"s1": maximum, "mt": split_max}
                for u in range(-1, UNITS - 1):
                    parts = list(range(RECIPS)) if u > 0 else []

                    def some_recips(count):
                        for n in parts[:count]:
                            recip_part(u - 1, n)
                            if n == RECIPS - 1:
                                normalise_attn(u - 1)
                        del parts[:count]

                    if 0 <= u < UNITS - 2 and u not in LO_BEFORE:
                        qk_to_lo(u + 2, 0)
                        some_recips(RECIPS_BETWEEN)
                        qk_to_lo(u + 2, 1)
                    for n, (what, *which) in enumerate(beside(u)):
                        if n in LO_BEFORE.get(u, ()):
                            qk_to_lo(u + 2, LO_BEFORE[u].index(n))
                        take[what](*which)
                        if u < 0 and n in TAKE_AFTER:
                            take_v(CT + 2 + TAKE_AFTER.index(n))
                        if n == len(beside(u)) - 1:
                            some_recips(RECIPS)
                        elif n >= RECIPS_FROM:
                            some_recips(1)
                for n in range(RECIPS):
                    recip_part(UNITS - 2, n)
                normalise_attn(UNITS - 2)
                for t in range(CT):
                    add_projected(t)
                chunk_variance(it, 1, 0)
                normalise_pair(it, 1, 0)
                normalise_pair(it, 1, 1)
                xt_to_lo(it, 1, 0)
                xt_to_lo(it, 1, 1)
                for n in range(RECIPS):
                    recip_part(UNITS - 1, n)
                normalise_attn(UNITS - 1)
                split_last()
                hidden_parts(0, 0)
                for t in range(CT, TT):
                    add_projected(t)
                chunk_variance(it, 1, 1)
                normalise_pair(it, 1, 2)
                normalise_pair(it, 1, 3)
                hidden_parts(0, 1)
                xt_to_lo(it, 1, 2)
                xt_to_lo(it, 1, 3)
                down_rows(0)
                for s in range(1, STEPS - 1):
                    for t in range(BT):
                        hidden_parts(s, t)
                    for d in downs_after(s):
                        down_rows(d)
                dve.wait_ge(rows_drained, it * ROWS + ROWS - CT)
                chunk_stats(it + 1, 0, b + layer + 1)
                normalise_pair(it + 1, 0, 0)
                normalise_pair(it + 1, 0, 1)
                hidden_parts(STEPS - 1, 0)
                hidden_parts(STEPS - 1, 1)
                xt_to_lo(it + 1, 0, 0)
                xt_to_lo(it + 1, 0, 1)
                down_rows(STEPS - 1)
                dve.wait_ge(rows_drained, it * ROWS + ROWS)

            chunk_stats(0, 0, 1)
            normalise_pair(0, 0, 0)
            normalise_pair(0, 0, 1)
            xt_to_lo(0, 0, 0)
            xt_to_lo(0, 0, 1)
            with dve.Fori(0, BATCH) as b:
                with dve.Fori(0, LAYERS) as layer:
                    iteration(b * LAYERS + layer, b, layer)

        @block.tensor
        def _(pe):
            pe.wait_ge(const_ready, CONSTS)
            pe.wait_ge(ring_drained, RING_CREDIT)

            def transpose_pair(it, ln, r):
                name = (f"ln{ln + 1}", r)
                pe.wait_ge(ring_drained, buffer_free(it, name))
                pe.wait_ge(xn_ready, it * 2 * TT + ln * TT + 2 * r + 2)
                for t in range(2):
                    for k in range(KT):
                        cols = slice(k * P, (k + 1) * P)
                        ins = pe.transpose(buffer_of(name)[:, t, cols], xn_tile(2 * r + t)[:, cols], ident[:, :])
                ins.then_inc(ring_full, 1)

            def iteration(it):
                def three(dst, terms, first=True, last=True):
                    n = len(terms)
                    for k, (ah, al, bh, bl) in enumerate(terms):
                        pe.matmul(dst, ah, bh, start=first and k == 0, stop=False)
                        pe.matmul(dst, ah, bl, start=False, stop=False)
                        ins = pe.matmul(dst, al, bh, start=False, stop=last and k == n - 1)
                    return ins

                BUT_LAST, LAST_GROUP = range(GROUPS - 1), range(GROUPS - 1, GROUPS)

                def xt_part(k, cols):
                    return xt_hi[:, k, cols], xt_lo[:, k, cols]

                def value_part(t, k):
                    if k == 0:
                        if t < CT:
                            pe.wait_ge(ring_drained, buffer_free(it, ("v", t)))
                        pe.wait_ge(ring_drained, drained(it, ("ln1", t // 2)))
                        pe.wait_ge(w_split, it * SLOTS + V_SLOTS[1] + 1)
                    dst = buffer_of(("v", t))[:, 0, :] if t < CT else bank[t - CT][:, :]
                    terms = [(*xt_part(k, slice(t * P, (t + 1) * P)),
                              *w_part(V_SLOTS[k // 2], slice(k % 2 * DIM, (k % 2 + 1) * DIM)))]
                    ins = three(dst, terms, k == 0, k == KT - 1)
                    if k == KT - 1:
                        ins.then_inc(ring_full if t < CT else side_full, 1)

                def value_tile(t):
                    for k in range(KT):
                        value_part(t, k)

                def project(u, w, half):
                    g, c = unit(u)
                    if half == 0:
                        if u == 2:
                            pe.wait_ge(side_taken, side_done(it, ("v", TT - 2 + w)))
                        elif u in SIDE_UNITS:
                            pe.wait_ge(ring_drained, drained(it, ("s1", u - 2, GH * CT - 2 + w)))
                        else:
                            pe.wait_ge(ring_drained, buffer_free(it, ("qk"[w], u)))
                        if w == 0:
                            pe.wait_ge(ring_drained, drained(it, ("ln1", 2 * c + 1)))
                            pe.wait_ge(w_split, it * SLOTS + QK_SLOT0 + g + 1)
                    cols = slice(c * CHUNK, (c + 1) * CHUNK)
                    terms = [(*w_part(QK_SLOT0 + g, slice((2 * k + w) * P, (2 * k + w + 1) * P)), *xt_part(k, cols))
                             for k in range(half * KT // 2, (half + 1) * KT // 2)]
                    ins = three(projected(u, w), terms, half == 0, half == 1)
                    if half == 1:
                        ins.then_inc(side_full if u in SIDE_UNITS else ring_full, 1)

                def keys_of(u, chunk):
                    return k_buffer(u - unit(u)[1] + chunk)

                def scores(u, s):
                    _, c = unit(u)
                    h, t = divmod(s, CT)
                    if t == 0:
                        pe.wait_ge(kq_stacked[u % 2][h], stacked(it, u, len(STACKED)))
                    pe.wait_ge(ring_drained, buffer_free(it, ("s1", u, s)))
                    q = q_stack[0:3 * HEAD, q_buffer(u), h, t * P:(t + 1) * P]
                    for kc in range(c + 1):
                        n = CHUNK if kc < c else (t + 1) * P
                        ins = pe.matmul(buffer_of(("s1", u, s))[:, kc, 0:n], q,
                                        k_stack[0:3 * HEAD, keys_of(u, kc), h, 0:n], start=True, stop=True)
                    ins.then_inc(ring_full, 1)

                def transpose_max(u):
                    pe.wait_ge(ring_drained, buffer_free(it, ("mt", u)))
                    pe.wait_ge(ring_drained, drained(it, ("s1", u, GH * CT - 1)))
                    pe.transpose(buffer_of(("mt", u))[0:GH * CT, 0, 0:P], row_max[:, u % 2, :], ident[:, :]
                                 ).then_inc(ring_full, 1)

                def scores_t(u, j, h):
                    _, c = unit(u)
                    n = GH * (J_BASE[u] + j) + h
                    off = max(0, j - CT * c) * P
                    if u == 0 and j == 0 and h == 0:
                        pe.wait_ge(side_taken, side_done(it, ("v", TT - 1)))
                    if j == 0 and h == 0:
                        pe.wait_ge(max_stacked[u % 2], stacked(it, u, 2))
                        if u == 2:
                            pe.wait_ge(ones_ready, it + 1)
                    if n >= 2:
                        pe.wait_ge(prob_ready, it * S2_STEPS + n - 1)
                    rows = slice(0, 3 * HEAD + 2)
                    pe.matmul(bank[n % 2][:, off:], k_stack[rows, keys_of(u, j // CT), h, j % CT * P:(j % CT + 1) * P],
                              q_stack[rows, q_buffer(u), h, off:], start=True, stop=True).then_inc(s2_full, 1)

                def weigh(u, j, what):
                    g, c = unit(u)
                    step = J_BASE[u] + j
                    d = j - CT * c
                    off = max(0, d) * P
                    if what == "values":
                        pe.wait_ge(prob_ready, it * S2_STEPS + GH * (step + 1))
                        if d >= 0:
                            pe.wait_ge(mask_done, it * UNITS * CT + u * CT + d + 1)
                        if j == 0 and not u:
                            pe.wait_ge(side_taken, side_done(it, ("k", 2)))
                        if j == 0 and u:
                            pe.wait_ge(evacuated, it * UNITS + u)
                    for h in range(GH):
                        rows = slice(h * HEAD, (h + 1) * HEAD)
                        dst, a = ((out_bank, v[:, j, g * P + h * HEAD:g * P + (h + 1) * HEAD]) if what == "values"
                                  else (den_bank, ones[:, :]))
                        ins = pe.matmul(dst[rows, off:], a, prob[:, step % 2, h, off:], start=j == 0,
                                        stop=j == key_tiles(u) - 1, tile_position=(0, h * HEAD))
                    if what == "sums":
                        ins.then_inc(pv_done, 1)

                def project_out(t, groups=range(GROUPS)):
                    name, c = ("op", t), t // CT
                    if groups[0] == 0:
                        pe.wait_ge(ring_drained, buffer_free(it, name))
                        if t == 0:
                            pe.wait_ge(attn_split, it * (UNITS - 1) + UNITS - 3)
                            pe.wait_ge(w_split, it * SLOTS + WO_SLOT0 + 2)
                    if t == 0 and groups[-1] == GROUPS - 1:
                        pe.wait_ge(attn_split, it * (UNITS - 1) + UNITS - 1)
                    if t == CT and groups[-1] == GROUPS - 1:
                        pe.wait_ge(last_split, it + 1)
                    cols = slice(t * P, (t + 1) * P)
                    terms = [(*xt_part(g, cols), *w_part(WO_SLOT0 + g // 2, slice(g % 2 * DIM, (g % 2 + 1) * DIM)))
                             for g in groups]
                    ins = three(buffer_of(name)[:, 0, :], terms, groups[0] == 0, groups[-1] == GROUPS - 1)
                    if groups[-1] == GROUPS - 1:
                        ins.then_inc(ring_full, 1)

                def gate_up(s, t):
                    b, c = divmod(s, CHUNKS)
                    cols = slice(c * CHUNK, (c + 1) * CHUNK)
                    if t == 0 and b == 0:
                        pe.wait_ge(ring_drained, drained(it, ("ln2", 2 * c + 1)))
                    if t == 0 and c == 0:
                        pe.wait_ge(w_split, it * SLOTS + FFN_SLOT0 + 3 * b + 2)
                    pe.wait_ge(ring_drained, buffer_free(it, ("gu", s, t)))
                    for w in range(2):
                        terms = [(*w_part(FFN_SLOT0 + 3 * b + w, slice(k * BLOCK + t * P, k * BLOCK + (t + 1) * P)),
                                  *xt_part(k, cols)) for k in range(KT)]
                        ins = three(buffer_of(("gu", s, t))[:, w, :], terms)
                    ins.then_inc(ring_full, 1)

                def down(s):
                    b, c = divmod(s, CHUNKS)
                    pe.wait_ge(h_ready, it * HID_TILES + (s + 1) * BT)
                    if c == 0:
                        pe.wait_ge(w_split, it * SLOTS + FFN_SLOT0 + 3 * b + 3)
                    if s == 0:
                        pe.wait_ge(evacuated, it * UNITS + UNITS)
                    for t in range(CT):
                        row = s * CT + t
                        if s:
                            pe.wait_ge(rows_drained, it * ROWS + row - CT + 1)
                        tok = slice(t * P, (t + 1) * P)
                        terms = [(h_parts[:, s % 2, 0, i, tok], h_parts[:, s % 2, 1, i, tok],
                                  *w_part(FFN_SLOT0 + 3 * b + 2, slice(i * DIM, (i + 1) * DIM))) for i in range(BT)]
                        three(bank[t][:, :], terms).then_inc(rows_full, 1)

                for t in range(CT):
                    value_tile(t)
                def project_whole(u, w):
                    for half in range(2):
                        project(u, w, half)

                project_whole(0, 0)
                transpose_pair(it, 0, 2)
                project_whole(0, 1)
                transpose_pair(it, 0, 3)
                value_tile(CT)
                project_whole(1, 0)
                project_whole(1, 1)
                value_tile(CT + 1)
                run = {"s1": scores, "mt": transpose_max,
                       "op": lambda t: project_out(t, range(GROUPS) if t >= 2 else LAST_GROUP),
                       "ln2": lambda r: transpose_pair(it, 1, r)}
                for n, (what, *which) in enumerate(beside(-1)):
                    run[what](*which)
                    if n % 2 and n // 2 < 2 * KT:
                        value_part(CT + 2 + n // 2 // KT, n // 2 % KT)
                for u in range(UNITS):
                    def weigh_last():
                        if u:
                            weigh(u - 1, key_tiles(u - 1) - 1, "values")
                            weigh(u - 1, key_tiles(u - 1) - 1, "sums")

                    early = 0

                    def between(quarter):
                        nonlocal early
                        if u in BETWEEN:
                            for what, *which in beside(u)[early:early + BETWEEN[u][quarter]]:
                                run[what](*which)
                            early += BETWEEN[u][quarter]

                    if u + 2 < UNITS:
                        project(u + 2, 0, 0)
                        weigh_last()
                        between(0)
                        project(u + 2, 0, 1)
                        between(1)
                        scores_t(u, 0, 0)
                        scores_t(u, 0, 1)
                        project(u + 2, 1, 0)
                        between(2)
                        scores_t(u, 0, 2)
                        scores_t(u, 0, 3)
                        project(u + 2, 1, 1)
                        between(3)
                    else:
                        if u == UNITS - 1:
                            project_out(0, BUT_LAST)
                            weigh_last()
                            project_out(1, BUT_LAST)
                        scores_t(u, 0, 0)
                        scores_t(u, 0, 1)
                        if u < UNITS - 1:
                            weigh_last()
                        scores_t(u, 0, 2)
                        scores_t(u, 0, 3)
                    point = 0
                    for j in range(1, key_tiles(u)):
                        for half, what in enumerate(("values", "sums")):
                            for own in range(2):
                                if own == 0:
                                    scores_t(u, j, 2 * half)
                                    scores_t(u, j, 2 * half + 1)
                                else:
                                    weigh(u, j - 1, what)
                                for (name, *which), at in zip(beside(u)[early:], points(u)):
                                    if at == point:
                                        run[name](*which)
                                point += 1
                weigh(UNITS - 1, key_tiles(UNITS - 1) - 1, "values")
                weigh(UNITS - 1, key_tiles(UNITS - 1) - 1, "sums")
                gate_up(0, 0)
                for groups in (BUT_LAST, LAST_GROUP):
                    for t in (CT, CT + 1):
                        project_out(t, groups)
                for t in range(CT + 2, TT):
                    project_out(t)
                gate_up(0, 1)
                transpose_pair(it, 1, 2)
                transpose_pair(it, 1, 3)
                down(0)
                for s in range(1, STEPS - 1):
                    for t in range(BT):
                        gate_up(s, t)
                    for d in downs_after(s):
                        down(d)
                for t in range(BT):
                    gate_up(STEPS - 1, t)
                transpose_pair(it + 1, 0, 0)
                transpose_pair(it + 1, 0, 1)
                down(STEPS - 1)

            transpose_pair(0, 0, 0)
            transpose_pair(0, 0, 1)
            with pe.Fori(0, BATCH * LAYERS) as it:
                iteration(it)


def lay_out(np, L0_attn_a_x, L0_attn_a_W_qkv, L0_attn_a_b_qkv, L0_attn_a_W_out, L0_attn_a_b_out, L0_attn_b_w_qkv,
            L0_attn_b_b_qkv, L0_attn_b_w_proj, L0_attn_b_b_proj, L0_ffn_w_gate, L0_ffn_w_up, L0_ffn_w_down):
    def row_pairs(w):
        return np.asarray(w).reshape(2, 2, P, DIM).transpose(0, 2, 1, 3).reshape(2, P, SLOT)

    def attn_slots(qkv, proj):
        q, k = (qkv[:, n * DIM:(n + 1) * DIM].reshape(KT, P, GROUPS, 1, P) for n in range(2))
        qk = np.concatenate([q, k], 3).transpose(2, 1, 0, 3, 4).reshape(GROUPS, P, SLOT)
        return np.concatenate([row_pairs(qkv[:, 2 * DIM:]), qk, row_pairs(proj)])

    def column_blocks(w):
        return w.reshape(KT, P, BLOCKS, BLOCK).transpose(2, 1, 0, 3).reshape(BLOCKS, 1, P, SLOT)

    down = L0_ffn_w_down.T.reshape(BLOCKS, 1, BT, P, DIM).transpose(0, 1, 3, 2, 4).reshape(BLOCKS, 1, P, SLOT)
    ffn = np.concatenate([column_blocks(L0_ffn_w_gate.T), column_blocks(L0_ffn_w_up.T), down], 1)
    qkv_biases = (L0_attn_a_b_qkv, L0_attn_b_b_qkv)
    return {
        "x_in": L0_attn_a_x,
        "attn_w": np.stack([attn_slots(L0_attn_a_W_qkv.T, L0_attn_a_W_out.T),
                            attn_slots(L0_attn_b_w_qkv, L0_attn_b_w_proj)]),
        "ffn_w": ffn.reshape(3 * BLOCKS, P, SLOT),
        "qk_bias": np.stack([b[:2 * DIM].reshape(2, GROUPS, P).transpose(2, 0, 1) for b in qkv_biases]),
        "row_bias": np.stack([np.stack([b[2 * DIM:], o])
                              for b, o in zip(qkv_biases, (L0_attn_a_b_out, L0_attn_b_b_proj))]),
    }


def kernel(**inputs):
    import numpy as np
    import concourse.bacc as bacc
    from concourse.bass_utils import run_bass_kernel_spmd

    nc = bacc.Bacc("TRN2", target_bir_lowering=False, num_devices=1)
    laid = {n: np.ascontiguousarray(a) for n, a in lay_out(np, **{n: np.asarray(a) for n, a in inputs.items()}).items()}
    args = [nc.dram_tensor(n, a.shape, mybir.dt.from_np(a.dtype), kind="ExternalInput").ap() for n, a in laid.items()]
    out = nc.dram_tensor("out", (BATCH, TOKENS, DIM), F32, kind="ExternalOutput").ap()
    block_kernel(nc, *args, out)
    r = run_bass_kernel_spmd(nc, [laid], core_ids=[0])
    return r.results[0]["out"]
```
